# Optimizing a Trainium2 kernel written in Bass

```python
import numpy as np
import jax
import jax.numpy as jnp

def _softmax(x, axis=-1):
    return jax.nn.softmax(x, axis=axis)

def _gelu(x):
    return jax.nn.gelu(x, approximate=True)

def _silu(x):
    return jax.nn.silu(x)

def _sigmoid(x):
    return jax.nn.sigmoid(x)

def _layernorm(x, axis=-1, eps=1e-05):
    m = jnp.mean(x, axis=axis, keepdims=True)
    v = jnp.var(x, axis=axis, keepdims=True)
    return (x - m) / jnp.sqrt(v + eps)

def _scatter_add(tgt, idx, src, axis=0):
    return tgt.at[idx].add(src)

def _segment_sum(src, seg, n):
    return jax.ops.segment_sum(src, seg, n)
kernel_name = 'mk_xattn_ffn_d1_seqx_r8_817af8'

def setup_inputs(seed: int=0):
    np.random.seed(seed)
    _w = jnp.asarray

    def _rec_inputs():
        import jax
        import jax.numpy as jnp
        _rk = jax.random.key(seed)
        x = -0.0005207 + 1.001 * jax.random.normal(jax.random.fold_in(_rk, 1), (8, 256, 128), jnp.float32)
        _lenS = 256 - jax.random.randint(jax.random.fold_in(_rk, 7), (8,), 0, max(1, 256 // 4) + 1, jnp.int32)
        _lenS2 = 256 - jax.random.randint(jax.random.fold_in(_rk, 8), (8,), 0, max(1, 256 // 4) + 1, jnp.int32)
        _ctx_1024P = jax.random.normal(jax.random.fold_in(_rk, 11), (8, 16, 128), jnp.float32)
        _ctx_1024c = jax.random.dirichlet(jax.random.fold_in(_rk, 511), 0.3 * jnp.ones((16,), jnp.float32), (8, 256))
        _ctx_1024t = jnp.einsum('bsk,bkd->bsd', _ctx_1024c, _ctx_1024P)
        _ctx_1024t = _ctx_1024t * jax.lax.rsqrt(jnp.mean(jnp.square(_ctx_1024t)) + 1e-12) * 0.953939
        ctx_1024 = -0.000514642 + 1.00011 * (_ctx_1024t + 0.3 * jax.random.normal(jax.random.fold_in(_rk, 611), (8, 256, 128), jnp.float32))
        return (x, ctx_1024)
    x, ctx_1024 = _rec_inputs()

    def _L0_xattn_setup():
        import jax, jax.numpy as jnp
        import numpy as np
        DIM = 128
        HEADS = 8
        HEAD_DIM = DIM // HEADS
        TAU = HEAD_DIM ** 0.5
        BS, SEQ = (1, 256)
        key = jax.random.key(seed)
        kq, kk, kv, kb = jax.random.split(key, 4)
        q = jax.random.normal(kq, (BS, SEQ, DIM), jnp.float32)
        k = jax.random.normal(kk, (BS, SEQ, DIM), jnp.float32)
        v = jax.random.normal(kv, (BS, SEQ, DIM), jnp.float32)
        Wi_w = jnp.zeros((HEADS, 3 * DIM), jnp.float32)
        Wi_b = 0.1 * jax.random.normal(kb, (HEADS,), jnp.float32)
        Wf_w = jnp.zeros((HEADS, 3 * DIM), jnp.float32)
        Wf_b = jnp.linspace(3.0, 6.0, HEADS, dtype=jnp.float32)
        gn_w = jnp.ones((DIM,), jnp.float32)
        gn_b = jnp.zeros((DIM,), jnp.float32)
        return {'q': q, 'k': k, 'v': v, 'Wi_w': Wi_w, 'Wi_b': Wi_b, 'Wf_w': Wf_w, 'Wf_b': Wf_b, 'gn_w': gn_w, 'gn_b': gn_b}
    _L0_xattn_all = _L0_xattn_setup()
    _L0_xattn_in = {k: v for k, v in _L0_xattn_all.items() if k in ('Wi_w', 'Wi_b', 'Wf_w', 'Wf_b', 'gn_w', 'gn_b')}
    del _L0_xattn_all

    def _L0_ffn_setup():
        import jax, jax.numpy as jnp
        import numpy as np
        D = 128
        F = 128
        E = 8
        K = 2
        B, T = (2, 256)

        def _moe_forward(x, router_w, w1, w2, shared_gate_up, shared_down, shared_gate_w):
            b, t, d = x.shape
            xf = x.reshape(-1, d)
            n = xf.shape[0]
            logits = xf @ router_w
            probs = jax.nn.softmax(logits, axis=-1)
            topw, topi = jax.lax.top_k(probs, K)
            combine = jnp.zeros((n, E), dtype=probs.dtype).at[jnp.arange(n)[:, None], topi].add(topw)
            h = jax.nn.silu(jnp.einsum('nd,edf->nef', xf, w1))
            ye = jnp.einsum('nef,efd->ned', h, w2)
            routed = jnp.einsum('ne,ned->nd', combine, ye)
            gu = xf @ shared_gate_up
            gate, up = (gu[:, :F], gu[:, F:])
            shared = jax.nn.silu(gate) * up @ shared_down
            shared = jax.nn.sigmoid(xf @ shared_gate_w) * shared
            return (routed + shared).reshape(b, t, d)
        key = jax.random.key(seed)
        ks = jax.random.split(key, 7)
        std = 0.02
        x = jax.random.normal(ks[0], (B, T, D), dtype=jnp.float32)
        router_w = jax.random.normal(ks[1], (D, E), dtype=jnp.float32) * std
        w1 = jax.random.normal(ks[2], (E, D, F), dtype=jnp.float32) * std
        w2 = jax.random.normal(ks[3], (E, F, D), dtype=jnp.float32) * std
        shared_gate_up = jax.random.normal(ks[4], (D, 2 * F), dtype=jnp.float32) * std
        shared_down = jax.random.normal(ks[5], (F, D), dtype=jnp.float32) * std
        shared_gate_w = jax.random.normal(ks[6], (D, 1), dtype=jnp.float32) * std
        return {'x': x, 'router_w': router_w, 'w1': w1, 'w2': w2, 'shared_gate_up': shared_gate_up, 'shared_down': shared_down, 'shared_gate_w': shared_gate_w}
    _L0_ffn_all = _L0_ffn_setup()
    _L0_ffn_in = {k: v for k, v in _L0_ffn_all.items() if k in ('router_w', 'w1', 'w2', 'shared_gate_up', 'shared_down', 'shared_gate_w')}
    del _L0_ffn_all
    return {'x': x, 'ctx_1024': ctx_1024, 'L0_xattn_Wi_w': _L0_xattn_in['Wi_w'], 'L0_xattn_Wi_b': _L0_xattn_in['Wi_b'], 'L0_xattn_Wf_w': _L0_xattn_in['Wf_w'], 'L0_xattn_Wf_b': _L0_xattn_in['Wf_b'], 'L0_xattn_gn_w': _L0_xattn_in['gn_w'], 'L0_xattn_gn_b': _L0_xattn_in['gn_b'], 'L0_ffn_router_w': _L0_ffn_in['router_w'], 'L0_ffn_w1': _L0_ffn_in['w1'], 'L0_ffn_w2': _L0_ffn_in['w2'], 'L0_ffn_shared_gate_up': _L0_ffn_in['shared_gate_up'], 'L0_ffn_shared_down': _L0_ffn_in['shared_down'], 'L0_ffn_shared_gate_w': _L0_ffn_in['shared_gate_w']}

def reference(x, ctx_1024, L0_xattn_Wi_w, L0_xattn_Wi_b, L0_xattn_Wf_w, L0_xattn_Wf_b, L0_xattn_gn_w, L0_xattn_gn_b, L0_ffn_router_w, L0_ffn_w1, L0_ffn_w2, L0_ffn_shared_gate_up, L0_ffn_shared_down, L0_ffn_shared_gate_w):
    import jax
    import jax.numpy as jnp

    def _L0_xattn_ref(q, k, v, Wi_w, Wi_b, Wf_w, Wf_b, gn_w, gn_b):
        import jax, jax.numpy as jnp
        import numpy as np
        DIM = 128
        HEADS = 8
        HEAD_DIM = DIM // HEADS
        TAU = HEAD_DIM ** 0.5
        BS, SEQ = (1, 256)
        bs, seq, dim = q.shape
        gate_in = jnp.concatenate([q, k, v], axis=-1)
        itilde = jnp.einsum('bsd,hd->bhs', gate_in, Wi_w) + Wi_b[None, :, None]
        ftilde = jnp.einsum('bsd,hd->bhs', gate_in, Wf_w) + Wf_b[None, :, None]
        csum = jnp.cumsum(jax.nn.log_sigmoid(ftilde), axis=-1)
        Fmat = csum[..., :, None] - csum[..., None, :]
        mask = jnp.tril(jnp.ones((seq, seq), dtype=bool))
        F_act = jnp.where(mask, Fmat, -jnp.inf)
        Dtilde = F_act + itilde[..., None, :]
        max_d = jnp.max(Dtilde, axis=-1, keepdims=True)
        D = jnp.exp(Dtilde - max_d)
        qh = q.reshape(bs, seq, HEADS, HEAD_DIM).transpose(0, 2, 1, 3)
        kh = k.reshape(bs, seq, HEADS, HEAD_DIM).transpose(0, 2, 1, 3)
        vh = v.reshape(bs, seq, HEADS, HEAD_DIM).transpose(0, 2, 1, 3)
        Ctilde = jnp.einsum('bhid,bhjd->bhij', qh, kh) * D / TAU
        maxit = jnp.maximum(jnp.abs(jnp.sum(Ctilde, axis=-1, keepdims=True)), jnp.exp(-max_d))
        Htilde = jnp.einsum('bhij,bhjd->bhid', Ctilde, vh) / (maxit + 1e-06)
        x = Htilde.transpose(0, 2, 1, 3).reshape(bs * seq, HEADS, HEAD_DIM)
        mean = jnp.mean(x, axis=-1, keepdims=True)
        var = jnp.var(x, axis=-1, keepdims=True)
        xn = (x - mean) / jnp.sqrt(var + 1e-05)
        out = xn.reshape(bs * seq, DIM) * gn_w + gn_b
        return out.reshape(bs, seq, DIM)

    def _L0_ffn_ref(x, router_w, w1, w2, shared_gate_up, shared_down, shared_gate_w):
        import jax, jax.numpy as jnp
        import numpy as np
        D = 128
        F = 128
        E = 8
        K = 2
        B, T = (2, 256)

        def _moe_forward(x, router_w, w1, w2, shared_gate_up, shared_down, shared_gate_w):
            b, t, d = x.shape
            xf = x.reshape(-1, d)
            n = xf.shape[0]
            logits = xf @ router_w
            probs = jax.nn.softmax(logits, axis=-1)
            topw, topi = jax.lax.top_k(probs, K)
            combine = jnp.zeros((n, E), dtype=probs.dtype).at[jnp.arange(n)[:, None], topi].add(topw)
            h = jax.nn.silu(jnp.einsum('nd,edf->nef', xf, w1))
            ye = jnp.einsum('nef,efd->ned', h, w2)
            routed = jnp.einsum('ne,ned->nd', combine, ye)
            gu = xf @ shared_gate_up
            gate, up = (gu[:, :F], gu[:, F:])
            shared = jax.nn.silu(gate) * up @ shared_down
            shared = jax.nn.sigmoid(xf @ shared_gate_w) * shared
            return (routed + shared).reshape(b, t, d)
        return _moe_forward(x, router_w, w1, w2, shared_gate_up, shared_down, shared_gate_w)
    x = x + _L0_xattn_ref(_layernorm(x, axis=-1), ctx_1024, ctx_1024, L0_xattn_Wi_w, L0_xattn_Wi_b, L0_xattn_Wf_w, L0_xattn_Wf_b, L0_xattn_gn_w, L0_xattn_gn_b)
    x = x + _L0_ffn_ref(_layernorm(x, axis=-1), L0_ffn_router_w, L0_ffn_w1, L0_ffn_w2, L0_ffn_shared_gate_up, L0_ffn_shared_down, L0_ffn_shared_gate_w)
    return x

_drawn_inputs = setup_inputs


def setup_inputs(seed=0):
    import zlib

    import numpy as np

    out = dict(_drawn_inputs(seed))
    spreads = {'L0_xattn_Wi_w': (0.0, 0.1),
     'L0_xattn_Wf_w': (0.0, 0.1),
     'L0_xattn_gn_w': (1.0, 0.2),
     'L0_xattn_gn_b': (0.0, 0.1)}
    factors = {'L0_xattn_Wi_b': 64.0,
     'L0_ffn_router_w': 8.0,
     'L0_ffn_w1': 8.0,
     'L0_ffn_w2': 8.0,
     'L0_ffn_shared_gate_up': 8.0,
     'L0_ffn_shared_down': 8.0,
     'L0_ffn_shared_gate_w': 8.0}
    for name, (base, spread) in spreads.items():
        noise = np.random.default_rng([zlib.crc32(name.encode()), seed]).standard_normal(out[name].shape)
        drawn = base * np.exp(spread * noise) if base else spread * noise
        out[name] = jnp.asarray(drawn.astype(out[name].dtype))
    for name, factor in factors.items():
        out[name] = (out[name] * factor).astype(out[name].dtype)
    return out
```

```python
import numpy as np
from contextlib import ExitStack

import concourse.bass as bass
from concourse import mybir

B, S, D = 8, 256, 128
H, HD = 8, 16
E = 8
P = 128
C = 64
NT = B * S // P
TPB = S // P
NC = S // C
VW = HD + 1
HW = H * VW
BH = B * H
GRP = 4
NG = NT // GRP
EPS = 1e-5
NEG = -1e30

K_ID, K_BLK, K_TRI, K_IOTA, K_ONE, K_EPS, K_HALF = 0, 128, 136, 200, 208, 209, 210
K_COLS = K_HALF + 16


def xattn_moe(nc, x_d, ctx_d, wi_d, wf_d, bi_d, bf_d, gnw_d, gnb_d, router_d, gate_d, w1_d, w2_d, gu_d,
              down_d, const_d, sel_d, m_scratch, out_d):
    f32, f16, u32 = mybir.dt.float32, mybir.dt.float16, mybir.dt.uint32
    ALU, ACT, AX = mybir.AluOpType, mybir.ActivationFunctionType, mybir.AxisListType
    ctx = ExitStack()
    with ctx:
        def sb(name, shape, dt=f32):
            return ctx.enter_context(nc.sbuf_tensor(name, shape, dt))

        def sem(name):
            return ctx.enter_context(nc.semaphore(name))

        const = sb("const", [P, K_COLS])
        sel = sb("sel", [64, E + 1, P], f16)
        xs = sb("xs", [P, NT, D])
        cx = sb("cx", [P, NT, D + 2])
        q = sb("q", [P, NT, D])
        qT = sb("qT", [P, B * S])
        qT2 = sb("qT2", [P, 2, B * S], f16)
        kT2 = sb("kT2", [P, 2, B * S], f16)
        v2 = sb("v2", [P, 2, NT, H, VW], f16)
        wg = sb("wg", [2 * H, 3 * D])
        wgT = sb("wgT", [P, 3, 2 * H])
        wgs = sb("wgs", [P, 2, 2 * H])
        wg2 = sb("wg2", [P, 2, 2, 2 * H], f16)
        bi = sb("bi", [BH, 1])
        bf = sb("bf", [BH, 1])
        gnw = sb("gnw", [P, D])
        gnb = sb("gnb", [P, D])
        w1 = sb("w1", [P, E + 2, D])
        w12 = sb("w12", [P, 2, E + 2, D], f16)
        w2 = sb("w2", [P, E + 1, D])
        wr = sb("wr", [P, E + 1])
        wr2 = sb("wr2", [P, 2, E + 1], f16)
        st1 = sb("st1", [P, NT, 6])
        mv1 = sb("mv1", [P, NT, 2])
        ve1 = sb("ve1", [P, NT])
        rs1 = sb("rs1", [P, NT])
        gtok = sb("gtok", [P, 2, TPB, B, H])
        absf = sb("absf", [BH, S])
        ef = sb("ef", [BH, S])
        lf = sb("lf", [BH, S])
        mf = sb("mf", [BH, S])
        csum = sb("csum", [BH, S])
        gg = sb("gg", [BH, S])
        mm = sb("mm", [BH, S])
        md = sb("md", [BH, S])
        negR = sb("negR", [BH, NC])
        em = sb("em", [BH, S])
        wq = sb("wq", [BH, S])
        wk = sb("wk", [BH, NC - 1, S])
        tok = sb("tok", [P, 10, B, H])
        T_G, T_EM, T_WQ, T_WK = 0, 2, 4, 6
        qblk = sb("qblk", [P, 2, 2, H, S], f16)
        mb = sb("mb", [P, 2, TPB, H, C])
        dd = sb("dd", [P, 2, TPB, H, C])
        ct = sb("ct", [P, 2, TPB, H, C])
        ct2 = sb("ct2", [P, 2, 2, TPB, H, C], f16)
        kw = sb("kw", [P, 2, 4, D])
        cst = sb("cst", [P, 2, NC - 1, H, VW])
        ti = sb("ti", [P, TPB, H, VW])
        y = sb("y", [P, TPB, H, VW])
        ssum = sb("ssum", [P, TPB * H])
        rr = sb("rr", [P, TPB * H])
        r2 = sb("r2", [P, TPB * H])
        mean = sb("mean", [P, TPB * H])
        yc = sb("yc", [P, TPB * H, HD])
        sq = sb("sq", [P, TPB * H, HD])
        vs = sb("vs", [P, TPB * H])
        ve = sb("ve", [P, TPB * H])
        rstd = sb("rstd", [P, TPB * H])
        fac = sb("fac", [P, TPB * H])
        yn = sb("yn", [P, TPB, D])
        yw = sb("yw", [P, TPB, D])
        xg = sb("xg", [P, 2, TPB, D])
        x2 = sb("x2", [P, 2, TPB, D])
        st2 = sb("st2", [P, TPB, 6])
        mv2 = sb("mv2", [P, TPB, 2])
        ve2 = sb("ve2", [P, TPB])
        rs2 = sb("rs2", [P, TPB])
        xn = sb("xn", [P, TPB, D])
        xnT2 = sb("xnT2", [P, 2, S], f16)
        lg = sb("lg", [P, TPB, E + 1])
        top = sb("top", [P, TPB, 8])
        tix = sb("tix", [P, TPB, 8], u32)
        lm = sb("lm", [P, TPB, E + 1])
        ex = sb("ex", [P, TPB, E + 1])
        eq1 = sb("eq1", [P, TPB, E])
        eq2 = sb("eq2", [P, TPB, E])
        den = sb("den", [P, TPB, 2])
        rden = sb("rden", [P, TPB, 2])
        comb = sb("comb", [P, TPB, E + 1])
        cT2 = sb("cT2", [64, S], f16)
        hh = sb("hh", [P, 2, 2, S])
        up = sb("up", [P, S])
        hc = sb("hc", [P, 2, 2, S])
        yT = sb("yT", [P, S])
        ob = sb("ob", [P, 2, TPB, D])

        ident = const[:, K_ID:K_ID + P]
        blk8 = const[:, K_BLK:K_BLK + H]
        tri = const[:, K_TRI:K_TRI + C]
        iota = const[:, K_IOTA:K_IOTA + E]
        one = const[:, K_ONE:K_ONE + 1]
        neghalf = const[:, K_HALF:K_HALF + 16]

        bank = [ctx.enter_context(nc.psum_tensor(f"bank{i}", [P, 512], f32)) for i in range(8)]
        pS = bank[0:2]
        pP, pC, pY = bank[2], bank[3], bank[4]
        pH = bank[5:7]
        pB = bank[7]

        consts_in, gatew_in, gn_in, ffn_in = sem("consts_in"), sem("gatew_in"), sem("gn_in"), sem("ffn_in")
        x_in = [sem(f"x_in{g}") for g in range(NG)]
        ctx_in = [sem(f"ctx_in{g}") for g in range(NG)]
        m_out, m_in, q_in, out_done = sem("m_out"), [sem("m_in0"), sem("m_in1")], \
            [sem("q_in0"), sem("q_in1")], [sem("out_done0"), sem("out_done1")]
        zeros_set, ones_set = sem("zeros_set"), sem("ones_set")
        var1_ready, rstd1_ready, q_ready = sem("var1_ready"), sem("rstd1_ready"), sem("q_ready")
        qT_done, kT_done, qT_hi, kT_hi, qT_lo, kT_lo = (sem(n) for n in (
            "qT_done", "kT_done", "qT_hi", "kT_hi", "qT_lo", "kT_lo"))
        v_hi, v_lo = sem("v_hi"), sem("v_lo")
        wgT_done, wg_split = sem("wgT_done"), sem("wg_split")
        gates_done, gtok_ready, gateT_done = sem("gates_done"), sem("gtok_ready"), sem("gateT_done")
        abs_ready, ln_ready, act_chain = sem("abs_ready"), sem("ln_ready"), sem("act_chain")
        m_ready, negR_ready, md_ready, fac_ready = sem("m_ready"), sem("negR_ready"), sem("md_ready"), \
            sem("fac_ready")
        tokT_done, tok_ready = sem("tokT_done"), sem("tok_ready")
        w1_hi, w1_lo = sem("w1_hi"), sem("w1_lo")
        dve_chain, pool_chain = sem("dve_chain"), sem("pool_chain")
        kw_ready, expo_ready, decay_ready, xg_ready = sem("kw_ready"), sem("expo_ready"), \
            sem("decay_ready"), sem("xg_ready")
        scores_done, ct_ready, ct_hi, ct_lo = sem("scores_done"), sem("ct_ready"), sem("ct_hi"), sem("ct_lo")
        state_done, cst_ready, intra_done, inter_done, y_ready = sem("state_done"), sem("cst_ready"), \
            sem("intra_done"), sem("inter_done"), sem("y_ready")
        yc_ready, sq_ready, ve_ready, rstd_ready = sem("yc_ready"), sem("sq_ready"), sem("ve_ready"), \
            sem("rstd_ready")
        x2_ready, ve2_ready, rs2_ready, xn_ready = sem("x2_ready"), sem("ve2_ready"), sem("rs2_ready"), \
            sem("xn_ready")
        xnT_done, xnT_hi, xnT_lo = sem("xnT_done"), sem("xnT_hi"), sem("xnT_lo")
        logits_done, lg_ready, lm_ready, ex_ready, comb_ready = sem("logits_done"), sem("lg_ready"), \
            sem("lm_ready"), sem("ex_ready"), sem("comb_ready")
        combT_done, cT_ready = sem("combT_done"), sem("cT_ready")
        hid_done, cb_done, silu_ready, hc_ready, down_done = sem("hid_done"), sem("cb_done"), \
            sem("silu_ready"), sem("hc_ready"), sem("down_done")
        yT_ready, back_done, ob_ready = sem("yT_ready"), sem("back_done"), \
            sem("ob_ready")

        x_v = x_d.rearrange("b (t p) d -> p (b t) d", p=P)
        c_v = ctx_d.rearrange("b (t p) d -> p (b t) d", p=P)
        o_v = out_d.rearrange("b (t p) d -> p (b t) d", p=P)
        HSESS = E // 2 + 1
        block = ctx.enter_context(nc.Block())

        def store(sp, b):
            sp.wait_ge(ob_ready, b + 1)
            sp.dma_start(o_v[:, b * TPB:(b + 1) * TPB, :], ob[:, b % 2]).then_inc(out_done[b % 2], 16)

        def normalise(dve, g):
            dve.wait_ge(rstd1_ready, g + 1)
            for t in range(g * GRP, (g + 1) * GRP):
                ins = nc.vector.tensor_scalar(q[:, t], xs[:, t], mv1[:, t, 0:1], rs1[:, t:t + 1],
                                              ALU.subtract, ALU.mult)
            ins.then_inc(q_ready, 1)

        @block.sync
        def _(sp):
            sp.dma_start(xs[:, 0:GRP, :], x_v[:, 0:GRP, :]).then_inc(x_in[0], 16)
            sp.dma_start(cx[:, 0:GRP, 0:D], c_v[:, 0:GRP, :]).then_inc(ctx_in[0], 16)
            sp.dma_start(const[:, :], const_d).then_inc(consts_in, 16)
            for g in range(1, NG):
                a = g * GRP
                sp.dma_start(xs[:, a:a + GRP, :], x_v[:, a:a + GRP, :]).then_inc(x_in[g], 16)
                sp.dma_start(cx[:, a:a + GRP, 0:D], c_v[:, a:a + GRP, :]).then_inc(ctx_in[g], 16)
            sp.dma_start(wg[0:H, :], wi_d).then_inc(gatew_in, 16)
            sp.dma_start(wg[H:2 * H, :], wf_d).then_inc(gatew_in, 16)
            sp.dma_start(bi[:, :], bi_d).then_inc(gatew_in, 16)
            sp.dma_start(bf[:, :], bf_d).then_inc(gatew_in, 16)
            sp.dma_start(gnw[:, :], gnw_d).then_inc(gn_in, 16)
            sp.dma_start(gnb[:, :], gnb_d).then_inc(gn_in, 16)
            sp.dma_start(w1[:, 0:E, :], w1_d.rearrange("e d f -> d e f")).then_inc(ffn_in, 16)
            sp.dma_start(w1[:, E:E + 2, :], gu_d.rearrange("d (g f) -> d g f", g=2)).then_inc(ffn_in, 16)
            sp.dma_start(w2[:, 0:E, :], w2_d.rearrange("e f d -> f e d")).then_inc(ffn_in, 16)
            sp.dma_start(w2[:, E, :], down_d).then_inc(ffn_in, 16)
            sp.dma_start(wr[:, 0:E], router_d).then_inc(ffn_in, 16)
            sp.dma_start(wr[:, E:E + 1], gate_d).then_inc(ffn_in, 16)
            sp.dma_start(sel[:, :, :], sel_d).then_inc(ffn_in, 16)

            def q_planes(b):
                g = b * TPB // GRP
                sp.wait_ge(zeros_set, 1)
                sp.wait_ge(qT_hi, g + 1)
                sp.wait_ge(qT_lo, g + 1)
                if b >= 2:
                    sp.wait_ge(scores_done, TPB * (b - 1))
                for h in range(H):
                    r = slice(h * HD, (h + 1) * HD)
                    sp.dma_start(qblk[r, b % 2, :, h, :], qT2[r, :, b * S:(b + 1) * S])\
                        .then_inc(q_in[b % 2], 16)

            def m_rows(b):
                if b >= 2:
                    sp.wait_ge(expo_ready, b - 1)
                for half in range(2):
                    src = m_scratch[half::2, b * H:(b + 1) * H, :].rearrange("(o t) h i -> o t (h i)", o=1)\
                        .to_broadcast([C, TPB, H * C])
                    sp.dma_start(mb[half * C:(half + 1) * C, b % 2].rearrange("p t h i -> p t (h i)"),
                                 src).then_inc(m_in[b % 2], 16)

            q_planes(0)
            q_planes(1)
            sp.wait_ge(m_ready, 1)
            sp.dma_start(m_scratch.rearrange("n r i -> r n i"),
                         mm[:, :].rearrange("r (n i) -> r n i", n=NC)).then_inc(m_out, 16)
            sp.wait_ge(m_out, 16)
            m_rows(0)
            m_rows(1)
            for b in range(B):
                if b + 2 < B:
                    q_planes(b + 2)
                    m_rows(b + 2)
                if b >= 2:
                    store(sp, b - 2)
            for b in range(B - 2, B):
                store(sp, b)
            for k in range(2):
                sp.wait_ge(out_done[k], 16 * (B // 2))

        @block.gpsimd
        def _(pool):
            nc.gpsimd.memset(qblk[:, :, :, :, :].rearrange("p a b h s -> p (a b h s)").bitcast(f32), 0.0)\
                .then_inc(zeros_set, 1)
            nc.gpsimd.memset(cx[:, :, D:D + 2], 1.0).then_inc(ones_set, 1)
            nc.gpsimd.memset(v2[:, 0, :, :, HD:VW], 1.0).then_inc(ones_set, 1)
            nc.gpsimd.memset(v2[:, 1, :, :, HD:VW], 0.0).then_inc(ones_set, 1)
            nc.gpsimd.memset(wk[:, :, :], 0.0).then_inc(ones_set, 1)
            nc.gpsimd.memset(wq[:, 0:C], 0.0).then_inc(ones_set, 1)
            nc.gpsimd.memset(ti[0:C, 0, :, :], 0.0).then_inc(ones_set, 1)
            nc.gpsimd.memset(cT2[:, :], 0.0).then_inc(ones_set, 1)
            pool.wait_ge(consts_in, 16)
            for g in range(NG):
                pool.wait_ge(var1_ready, g + 1)
                s = slice(g * GRP, (g + 1) * GRP)
                nc.gpsimd.tensor_tensor(rs1[:, s], ve1[:, s], neghalf[:, 0:GRP], ALU.pow)\
                    .then_inc(rstd1_ready, 1)
            for g in range(NG):
                pool.wait_ge(qT_hi, g + 1)
                s = slice(g * GRP * P, (g + 1) * GRP * P)
                nc.gpsimd.tensor_tensor(qT2[:, 1, s], qT[:, s], qT2[:, 0, s], ALU.subtract)\
                    .then_inc(qT_lo, 1)
            pool.wait_ge(gn_in, 32)
            for g in range(NG):
                pool.wait_ge(v_hi, g + 1)
                for a in range(g * GRP, (g + 1) * GRP):
                    ins = nc.gpsimd.tensor_tensor(
                        v2[:, 1, a, :, 0:HD], cx[:, a, 0:D].rearrange("p (h d) -> p h d", h=H),
                        v2[:, 0, a, :, 0:HD], ALU.subtract)
                ins.then_inc(v_lo, 1)
            pool.wait_ge(w1_hi, 1)
            nc.gpsimd.tensor_tensor(w12[:, 1], w1[:, :, :], w12[:, 0], ALU.subtract).then_inc(w1_lo, 1)
            pool.wait_ge(tok_ready, 1)

            def attention(b):
                k = b % 2
                t0 = b * TPB
                if b >= 2:
                    pool.wait_ge(ct_ready, TPB * (b - 1))
                for t in range(TPB):
                    ins = nc.gpsimd.tensor_tensor(
                        dd[:, k, t], tri.rearrange("p (o i) -> p o i", o=1).to_broadcast([P, H, C]),
                        tok[:, T_G + t, b, :].rearrange("p (h o) -> p h o", o=1).to_broadcast([P, H, C]),
                        ALU.add)
                ins.then_inc(pool_chain, 1)
                pool.wait_ge(pool_chain, b + 1)
                pool.wait_ge(m_in[k], 32 * (b // 2 + 1))
                ddf = dd[:, k].rearrange("p t h i -> p (t h i)")
                nc.gpsimd.tensor_tensor(ddf, ddf, mb[:, k].rearrange("p t h i -> p (t h i)"),
                                        ALU.subtract).then_inc(expo_ready, 1)
                if b >= 2:
                    pool.wait_ge(state_done, b - 1)
                for v in range(4):
                    a = t0 + (1 if v == 3 else 0)
                    ins = nc.gpsimd.tensor_tensor(
                        kw[:, k, v].rearrange("p (h d) -> p h d", h=H),
                        cx[:, a, 0:D].rearrange("p (h d) -> p h d", h=H),
                        tok[:, T_WK + v, b, :].rearrange("p (h o) -> p h o", o=1).to_broadcast([P, H, HD]),
                        ALU.mult)
                ins.then_inc(kw_ready, 1)
                if b >= 2:
                    pool.wait_ge(x2_ready, b - 1)
                for t in range(TPB):
                    ins = nc.gpsimd.tensor_tensor(xg[:, k, t], xs[:, t0 + t], gnb[:, :], ALU.add)
                ins.then_inc(xg_ready, 1)

            def low_half(b):
                k = b % 2
                pool.wait_ge(ct_hi, b + 1)
                if b >= 2:
                    pool.wait_ge(intra_done, b - 1)
                nc.gpsimd.tensor_tensor(
                    ct2[:, k, 1].rearrange("p t h i -> p (t h i)"),
                    ct[:, k].rearrange("p t h i -> p (t h i)"),
                    ct2[:, k, 0].rearrange("p t h i -> p (t h i)"), ALU.subtract).then_inc(ct_lo, 1)

            attention(0)
            for b in range(B):
                low_half(b)
                if b + 1 < B:
                    attention(b + 1)
                pool.wait_ge(ve_ready, b + 1)
                nc.gpsimd.tensor_tensor(rstd[:, :], ve[:, :], neghalf, ALU.pow).then_inc(rstd_ready, 1)
                pool.wait_ge(ve2_ready, b + 1)
                nc.gpsimd.tensor_tensor(rs2[:, :], ve2[:, :], neghalf[:, 0:TPB], ALU.pow)\
                    .then_inc(rs2_ready, 1)

        @block.scalar
        def _(act):
            chain = [0]

            def link(ins):
                chain[0] += 1
                ins.then_inc(act_chain, 1)
                act.wait_ge(act_chain, chain[0])

            nc.scalar.preload_act_table_set("natural_log_exp_and_others")
            act.wait_ge(ones_set, 7)
            for g in range(NG):
                s = slice(g * GRP * P, (g + 1) * GRP * P)
                act.wait_ge(ctx_in[g], 16)
                a = slice(g * GRP, (g + 1) * GRP)
                for t in range(g * GRP, (g + 1) * GRP):
                    ins = nc.scalar.copy(v2[:, 0, t, :, 0:HD], cx[:, t, 0:D].rearrange("p (h d) -> p h d", h=H))
                ins.then_inc(v_hi, 1)
                act.wait_ge(kT_done, g + 1)
                nc.scalar.copy(kT2[:, 0, s], bank[2 + g % 2][:, :]).then_inc(kT_hi, 1)
            for g in range(NG):
                s = slice(g * GRP * P, (g + 1) * GRP * P)
                act.wait_ge(qT_done, g + 1)
                nc.scalar.copy(qT2[:, 0, s], bank[g % 2][:, :])
                nc.scalar.copy(qT[:, s], bank[g % 2][:, :]).then_inc(qT_hi, 1)
            act.wait_ge(gatew_in, 64)
            act.wait_ge(gateT_done, 1)
            gf = bank[6][0:BH, S:2 * S]
            nc.scalar.activation(absf[:, :], gf, ACT.Abs, bias=bf[:, :]).then_inc(abs_ready, 1)
            act.wait_ge(abs_ready, 1)
            link(nc.scalar.activation(ef[:, :], absf[:, :], ACT.Exp, scale=-1.0))
            nc.scalar.activation(lf[:, :], ef[:, :], ACT.Ln, bias=one[0:BH, :]).then_inc(ln_ready, 1)
            act.wait_ge(negR_ready, 1)
            for n in range(NC - 1):
                nc.scalar.activation(wk[:, n, 0:(n + 1) * C], gg[:, 0:(n + 1) * C], ACT.Exp,
                                     bias=negR[:, n:n + 1])
                nc.scalar.activation(wq[:, (n + 1) * C:(n + 2) * C], mm[:, (n + 1) * C:(n + 2) * C],
                                     ACT.Exp, bias=mm[:, (n + 1) * C - 1:(n + 1) * C], scale=-1.0)
            act.wait_ge(md_ready, 1)
            nc.scalar.activation(em[:, :], md[:, :], ACT.Exp, scale=-1.0).then_inc(fac_ready, 1)
            act.wait_ge(ffn_in, 16 * 7)
            nc.scalar.copy(w12[:, 0], w1[:, :, :]).then_inc(w1_hi, 1)

            def decay(b):
                act.wait_ge(expo_ready, b + 1)
                f = dd[:, b % 2].rearrange("p t h i -> p (t h i)")
                nc.scalar.activation(f, f, ACT.Exp).then_inc(decay_ready, 1)

            def ct_high(b):
                k = b % 2
                act.wait_ge(ct_ready, TPB * (b + 1))
                if b >= 2:
                    act.wait_ge(intra_done, b - 1)
                nc.scalar.copy(ct2[:, k, 0].rearrange("p t h i -> p (t h i)"),
                               ct[:, k].rearrange("p t h i -> p (t h i)")).then_inc(ct_hi, 1)

            def xn_high(b):
                act.wait_ge(xnT_done, b + 1)
                if b >= 1:
                    act.wait_ge(hid_done, HSESS * b)
                nc.scalar.copy(xnT2[:, 0], pP[:, 0:S]).then_inc(xnT_hi, 1)

            def router_exp(b):
                act.wait_ge(lm_ready, b + 1)
                nc.scalar.activation(ex[:, :, :], lm[:, :, :], ACT.Exp).then_inc(ex_ready, 1)

            def silu(b, s):
                n = HSESS * b + s
                act.wait_ge(hid_done, n + 1)
                if n >= 2:
                    act.wait_ge(hc_ready, n - 1)
                w = 2 * S if s < HSESS - 1 else S
                nc.scalar.activation(hh[:, n % 2].rearrange("p e s -> p (e s)")[:, 0:w], pH[n % 2][:, 0:w],
                                     ACT.Silu).then_inc(silu_ready, 1)

            decay(0)
            for b in range(B + 1):
                if b >= 1:
                    xn_high(b - 1)
                if b < B:
                    ct_high(b)
                if b >= 1:
                    router_exp(b - 1)
                if b + 1 < B:
                    decay(b + 1)
                if b >= 1:
                    nc.scalar.preload_act_table_set("silu_and_others")
                for s in range(HSESS):
                    if b >= 1:
                        silu(b - 1, s)
                    if s == 1 and b < B:
                        act.wait_ge(yc_ready, b + 1)
                        nc.scalar.activation(sq[:, :, :], yc[:, :, :], ACT.Square).then_inc(sq_ready, 1)
                if b >= 1:
                    act.wait_ge(down_done, HSESS * b)
                    nc.scalar.copy(yT[:, :], pY[:, 0:S]).then_inc(yT_ready, 1)
                if 1 <= b < B:
                    nc.scalar.preload_act_table_set("natural_log_exp_and_others")

        @block.tensor
        def _(pe):
            def three(out, lhs, rhs):
                pe_ins = None
                for i, (u, v) in enumerate(((0, 0), (1, 0), (0, 1))):
                    pe_ins = pe.matmul(out, lhs(u), rhs(v), start=(i == 0), stop=(i == 2))
                return pe_ins

            pe.wait_ge(consts_in, 16)
            for g in range(NG):
                pe.wait_ge(ctx_in[g], 16)
                if g >= 2:
                    pe.wait_ge(kT_lo, g - 1)
                for t in range(GRP):
                    ins = pe.transpose(bank[2 + g % 2][:, t * P:(t + 1) * P], cx[:, g * GRP + t, 0:D], ident)
                ins.then_inc(kT_done, 1)
            pe.wait_ge(gatew_in, 64)
            for i in range(3):
                ins = pe.transpose(bank[5][:, i * 16:(i + 1) * 16], wg[:, i * D:(i + 1) * D],
                                   ident[0:2 * H, 0:2 * H])
            ins.then_inc(wgT_done, 1)
            for g in range(NG):
                pe.wait_ge(q_ready, g + 1)
                if g >= 2:
                    pe.wait_ge(qT_hi, g - 1)
                for t in range(GRP):
                    ins = pe.transpose(bank[g % 2][:, t * P:(t + 1) * P], q[:, g * GRP + t, :], ident)
                ins.then_inc(qT_done, 1)
            pe.wait_ge(wg_split, 1)
            for g in range(NG):
                pe.wait_ge(qT_lo, g + 1)
                pe.wait_ge(kT_lo, g + 1)
                for t in range(g * GRP, (g + 1) * GRP):
                    o = bank[4][:, t * 16:(t + 1) * 16]
                    s = slice(t * P, (t + 1) * P)
                    for i, (src, u, v) in enumerate(((qT2, 0, 0), (qT2, 1, 0), (qT2, 0, 1),
                                                     (kT2, 0, 0), (kT2, 1, 0), (kT2, 0, 1))):
                        ins = pe.matmul(o, src[:, u, s], wg2[:, v, 0 if src is qT2 else 1],
                                        start=(i == 0), stop=(i == 5))
            ins.then_inc(gates_done, 1)
            pe.wait_ge(gtok_ready, 1)
            for i in range(2):
                for t in range(TPB):
                    ins = pe.transpose(bank[6][0:BH, (i * TPB + t) * P:(i * TPB + t + 1) * P],
                                       gtok[:, i, t].rearrange("p b h -> p (b h)"), ident)
            ins.then_inc(gateT_done, 1)
            pe.wait_ge(fac_ready, 1)
            pe.wait_ge(md_ready, 1)
            parts = [gg[:, 0:P], gg[:, P:S], em[:, 0:P], em[:, P:S], wq[:, 0:P], wq[:, P:S],
                     wk[:, 0, 0:P], wk[:, 1, 0:P], wk[:, 2, 0:P], wk[:, 2, P:S]]
            for i, part in enumerate(parts):
                o = bank[7] if i < 8 else bank[5]
                ins = pe.transpose(o[:, (i % 8) * BH:(i % 8 + 1) * BH], part, ident[0:BH, 0:BH])
            ins.then_inc(tokT_done, 1)

            def scores(b):
                k = b % 2
                pe.wait_ge(q_in[k], 16 * H * (b // 2 + 1))
                for t in range(TPB):
                    if b >= 1:
                        pe.wait_ge(ct_ready, TPB * (b - 1) + t + 1)
                    for i, (u, v) in enumerate(((0, 0), (1, 0), (0, 1))):
                        for half in range(2):
                            n = 2 * t + half
                            a = b * S + n * C
                            ins = pe.matmul(pS[t][half * C:(half + 1) * C, :], kT2[:, u, a:a + C],
                                            qblk[:, k, v, :, n * C:(n + 1) * C],
                                            start=(i == 0), stop=(i == 2))
                    ins.then_inc(scores_done, 1)

            def states(b):
                k = b % 2
                pe.wait_ge(kw_ready, b + 1)
                if b >= 1:
                    pe.wait_ge(y_ready, b)
                for n, vs_ in enumerate(((0,), (1,), (2, 3))):
                    for j, v in enumerate(vs_):
                        a = b * TPB + (1 if v == 3 else 0)
                        ins = pe.matmul(pC[:, n * (D + 1):(n + 1) * (D + 1)], kw[:, k, v],
                                        cx[:, a, 0:D + 1], start=(j == 0), stop=(j == len(vs_) - 1))
                ins.then_inc(state_done, 1)

            def intra(b):
                k = b % 2
                pe.wait_ge(ct_lo, b + 1)
                if b >= 1:
                    pe.wait_ge(lg_ready, b)
                for t in range(TPB):
                    for h in range(H):
                        for i, (u, v) in enumerate(((0, 0), (1, 0), (0, 1))):
                            for half in range(2):
                                r = slice(half * C, (half + 1) * C)
                                ins = pe.matmul(pP[r, t * HW + h * VW:t * HW + (h + 1) * VW],
                                                ct2[r, k, u, t, h, :], v2[r, v, b * TPB + t, h, :],
                                                start=(i == 0), stop=(i == 2))
                ins.then_inc(intra_done, 1)

            def inter(b):
                k = b % 2
                pe.wait_ge(cst_ready, b + 1)
                for n in range(1, NC):
                    t, half = n // 2, n % 2
                    a = b * S + n * C
                    ins = pe.matmul(pC[half * C:(half + 1) * C, t * HW:(t + 1) * HW], qT[:, a:a + C],
                                    cst[:, k, n - 1].rearrange("p h v -> p (h v)"), start=True, stop=True)
                ins.then_inc(inter_done, 1)

            def xn_turn(b):
                pe.wait_ge(xn_ready, b + 1)
                for t in range(TPB):
                    ins = pe.transpose(pP[:, t * P:(t + 1) * P], xn[:, t], ident)
                ins.then_inc(xnT_done, 1)

            def logits(b):
                pe.wait_ge(xnT_lo, b + 1)
                for t in range(TPB):
                    s = slice(t * P, (t + 1) * P)
                    ins = three(pP[:, t * (E + 1):(t + 1) * (E + 1)], lambda u: xnT2[:, u, s],
                                lambda v: wr2[:, v])
                ins.then_inc(logits_done, 1)

            def comb_turn(b):
                pe.wait_ge(comb_ready, b + 1)
                if b >= 1:
                    pe.wait_ge(ob_ready, b)
                for t in range(TPB):
                    ins = pe.transpose(pY[0:E + 1, t * P:(t + 1) * P], comb[:, t], ident)
                ins.then_inc(combT_done, 1)

            def hidden(b, s):
                n = HSESS * b + s
                if n >= 2:
                    pe.wait_ge(silu_ready, n - 1)
                    if (n - 2) % HSESS == HSESS - 1:
                        pe.wait_ge(hc_ready, n - 1)
                for j in range(2):
                    ins = three(pH[n % 2][:, j * S:(j + 1) * S], lambda u: w12[:, u, 2 * s + j],
                                lambda v: xnT2[:, v])
                ins.then_inc(hid_done, 1)
                if s == 0:
                    pe.wait_ge(cT_ready, b + 1)
                if n >= 1:
                    pe.wait_ge(hc_ready, n)
                for j in range(2 if s < HSESS - 1 else 1):
                    ins = pe.matmul(pB[:, j * S:(j + 1) * S], sel[:, 2 * s + j], cT2[:, :],
                                    start=True, stop=True)
                ins.then_inc(cb_done, 1)

            def down(b, s):
                n = HSESS * b + s
                pe.wait_ge(hc_ready, n + 1)
                for j in range(2 if s < HSESS - 1 else 1):
                    e = 2 * s + j
                    ins = pe.matmul(pY[:, 0:S], w2[:, e], hc[:, n % 2, j], start=(e == 0), stop=(e == E))
                ins.then_inc(down_done, 1)

            def back(b):
                pe.wait_ge(yT_ready, b + 1)
                for t in range(TPB):
                    ins = pe.transpose(pY[:, t * P:(t + 1) * P], yT[:, t * P:(t + 1) * P], ident)
                ins.then_inc(back_done, 1)

            pe.wait_ge(tok_ready, 1)
            pe.wait_ge(v_lo, NG)
            for b in range(B + 1):
                if b < B:
                    scores(b)
                if b >= 1:
                    xn_turn(b - 1)
                if b < B:
                    states(b)
                if b >= 1:
                    logits(b - 1)
                if b < B:
                    intra(b)
                    inter(b)
                if b >= 1:
                    comb_turn(b - 1)
                    for s in range(HSESS):
                        hidden(b - 1, s)
                        if s >= 1:
                            down(b - 1, s - 1)
                    down(b - 1, HSESS - 1)
                    back(b - 1)

        @block.vector
        def _(dve):
            chain = [0]

            def step(ins):
                chain[0] += 1
                ins.then_inc(dve_chain, 1)

            def settle():
                dve.wait_ge(dve_chain, chain[0])

            def link(ins):
                step(ins)
                settle()

            def over(ap, n):
                m = ap.shape[1]
                return ap.rearrange("p (m o) -> p m o", o=1).to_broadcast([ap.shape[0], m, n])

            V = nc.vector
            for g in range(NG):
                dve.wait_ge(x_in[g], 16)
                for t in range(g * GRP, (g + 1) * GRP):
                    step(V.bn_stats(st1[:, t], xs[:, t]))
                settle()
                for t in range(g * GRP, (g + 1) * GRP):
                    step(V.bn_aggr(mv1[:, t], st1[:, t]))
                settle()
                s = slice(g * GRP, (g + 1) * GRP)
                V.tensor_scalar(ve1[:, s], mv1[:, s, 1], EPS, None, ALU.add).then_inc(var1_ready, 1)
                if g >= 1:
                    normalise(dve, g - 1)
            normalise(dve, NG - 1)
            for g in range(NG):
                dve.wait_ge(kT_hi, g + 1)
                s = slice(g * GRP * P, (g + 1) * GRP * P)
                V.tensor_tensor(kT2[:, 1, s], bank[2 + g % 2][:, :], kT2[:, 0, s], ALU.subtract)\
                    .then_inc(kT_lo, 1)
            dve.wait_ge(wgT_done, 1)
            link(V.tensor_copy(wgT[:, :, :].rearrange("p i g -> p (i g)"), bank[5][:, 0:48]))
            step(V.tensor_copy(wgs[:, 0], wgT[:, 0]))
            link(V.tensor_tensor(wgs[:, 1], wgT[:, 1], wgT[:, 2], ALU.add))
            link(V.tensor_copy(wg2[:, 0], wgs[:, :, :]))
            V.tensor_tensor(wg2[:, 1], wgs[:, :, :], wg2[:, 0], ALU.subtract).then_inc(wg_split, 1)
            dve.wait_ge(gates_done, 1)
            src = bank[4][:, 0:2 * H * NT].rearrange("p (b t g h) -> p b t g h", b=B, t=TPB, g=2)
            for i in range(2):
                for t in range(TPB):
                    ins = V.tensor_copy(gtok[:, i, t], src[:, :, t, i, :])
            ins.then_inc(gtok_ready, 1)
            dve.wait_ge(abs_ready, 1)
            dve.wait_ge(gatew_in, 64)
            gi, gf = bank[6][0:BH, 0:S], bank[6][0:BH, S:2 * S]
            link(V.tensor_scalar(mf[:, :], gf, bf[:, :], 0.0, ALU.add, ALU.min))
            dve.wait_ge(ln_ready, 1)
            link(V.tensor_tensor_scan(csum[:, :], mf[:, :], lf[:, :], 0.0, ALU.add, ALU.subtract))
            link(V.scalar_tensor_tensor(gg[:, :], gi, bi[:, :], csum[:, :], ALU.add, ALU.subtract))
            V.tensor_tensor_scan(mm[:, :], gg[:, :], gg[:, :], -3e38, ALU.max, ALU.max).then_inc(m_ready, 1)
            dve.wait_ge(m_ready, 1)
            V.tensor_scalar(negR[:, :], mm[:, C - 1::C], -1.0, None, ALU.mult).then_inc(negR_ready, 1)
            V.tensor_tensor(md[:, :], csum[:, :], mm[:, :], ALU.add).then_inc(md_ready, 1)
            dve.wait_ge(tokT_done, 1)
            V.tensor_copy(tok[:, 0:8].rearrange("p i b h -> p (i b h)"), bank[7][:, :])
            V.tensor_copy(tok[:, 8:10].rearrange("p i b h -> p (i b h)"), bank[5][:, 0:2 * BH])\
                .then_inc(tok_ready, 1)
            dve.wait_ge(tok_ready, 1)
            dve.wait_ge(ffn_in, 16 * 7)
            link(V.tensor_copy(wr2[:, 0], wr[:, :]))
            link(V.tensor_tensor(wr2[:, 1], wr[:, :], wr2[:, 0], ALU.subtract))

            def scores_decay(b):
                k = b % 2
                dve.wait_ge(decay_ready, b + 1)
                if b >= 2:
                    dve.wait_ge(ct_lo, b - 1)
                for t in range(TPB):
                    dve.wait_ge(scores_done, TPB * b + t + 1)
                    V.scalar_tensor_tensor(ct[:, k, t].rearrange("p h i -> p (h i)"), pS[t][:, :],
                                           HD ** -0.5, dd[:, k, t].rearrange("p h i -> p (h i)"),
                                           ALU.mult, ALU.mult).then_inc(ct_ready, 1)

            def states(b):
                k = b % 2
                dve.wait_ge(state_done, b + 1)
                if b >= 2:
                    dve.wait_ge(inter_done, b - 1)
                for n in range(NC - 1):
                    o = n * (D + 1)
                    V.scalar_tensor_tensor(
                        cst[:, k, n, :, 0:HD], pC[:, o:o + D].rearrange("p (h d) -> p h d", h=H),
                        HD ** -0.5, over(blk8, HD), ALU.mult, ALU.mult)
                    ins = V.tensor_scalar(cst[:, k, n, :, HD], blk8, pC[:, o + D:o + D + 1], HD ** -0.5,
                                          ALU.mult, ALU.mult)
                ins.then_inc(cst_ready, 1)

            def gather(b):
                dve.wait_ge(inter_done, b + 1)
                step(V.tensor_tensor(ti[C:P, 0], pC[C:P, 0:HW].rearrange("p (h v) -> p h v", h=H),
                                     over(tok[C:P, T_WQ, b, :], VW), ALU.mult))
                link(V.tensor_tensor(ti[:, 1], pC[:, HW:2 * HW].rearrange("p (h v) -> p h v", h=H),
                                     over(tok[:, T_WQ + 1, b, :], VW), ALU.mult))
                V.tensor_tensor(y[:, :].rearrange("p t h v -> p (t h v)"), pP[:, 0:2 * HW],
                                ti[:, :].rearrange("p t h v -> p (t h v)"), ALU.add).then_inc(y_ready, 1)
                dve.wait_ge(y_ready, b + 1)
                yv = y[:, :].rearrange("p t h v -> p (t h) v")
                step(V.tensor_reduce(mean[:, :], yv[:, :, 0:HD], AX.X, ALU.add))
                for t in range(TPB):
                    step(V.scalar_tensor_tensor(ssum[:, t * H:(t + 1) * H], y[:, t, :, HD], -1.0,
                                                tok[:, T_EM + t, b, :], ALU.mult, ALU.max))
                settle()
                step(V.tensor_tensor(ssum[:, :].rearrange("p (t h) -> p t h", t=TPB), y[:, :, :, HD],
                                     ssum[:, :].rearrange("p (t h) -> p t h", t=TPB), ALU.max))
                link(V.tensor_scalar(mean[:, :], mean[:, :], 1.0 / HD, None, ALU.mult))
                link(V.tensor_scalar(ssum[:, :], ssum[:, :], 1e-6, None, ALU.add))
                V.tensor_tensor(yc[:, :, :], yv[:, :, 0:HD], over(mean[:, :], HD), ALU.subtract)\
                    .then_inc(yc_ready, 1)
                link(V.reciprocal(rr[:, :], ssum[:, :]))
                link(V.tensor_tensor(r2[:, :], rr[:, :], rr[:, :], ALU.mult))

            def variance(b):
                dve.wait_ge(sq_ready, b + 1)
                link(V.tensor_reduce(vs[:, :], sq[:, :, :], AX.X, ALU.add))
                link(V.scalar_tensor_tensor(ve[:, :], vs[:, :], 1.0 / HD, r2[:, :], ALU.mult, ALU.mult))
                V.tensor_scalar(ve[:, :], ve[:, :], EPS, None, ALU.add).then_inc(ve_ready, 1)

            def group_norm(b):
                k = b % 2
                dve.wait_ge(rstd_ready, b + 1)
                dve.wait_ge(xg_ready, b + 1)
                link(V.tensor_tensor(fac[:, :], rstd[:, :], rr[:, :], ALU.mult))
                link(V.tensor_tensor(yn[:, :, :].rearrange("p t (h d) -> p (t h) d", h=H), yc[:, :, :],
                                     over(fac[:, :], HD), ALU.mult))
                link(V.tensor_tensor(yw[:, :, :], yn[:, :, :],
                                     gnw[:, :].rearrange("p (o d) -> p o d", o=1).to_broadcast([P, TPB, D]),
                                     ALU.mult))
                V.tensor_tensor(x2[:, k], yw[:, :, :], xg[:, k], ALU.add).then_inc(x2_ready, 1)
                dve.wait_ge(x2_ready, b + 1)
                for t in range(TPB):
                    step(V.bn_stats(st2[:, t], x2[:, k, t]))
                settle()
                for t in range(TPB):
                    step(V.bn_aggr(mv2[:, t], st2[:, t]))
                settle()
                V.tensor_scalar(ve2[:, :], mv2[:, :, 1], EPS, None, ALU.add).then_inc(ve2_ready, 1)

            def layer_norm(b):
                dve.wait_ge(rs2_ready, b + 1)
                for t in range(TPB):
                    ins = V.tensor_scalar(xn[:, t], x2[:, b % 2, t], mv2[:, t, 0:1], rs2[:, t:t + 1],
                                          ALU.subtract, ALU.mult)
                ins.then_inc(xn_ready, 1)

            def xn_low(b):
                dve.wait_ge(xnT_hi, b + 1)
                V.tensor_tensor(xnT2[:, 1], pP[:, 0:S], xnT2[:, 0], ALU.subtract).then_inc(xnT_lo, 1)

            def route(b):
                dve.wait_ge(logits_done, b + 1)
                V.tensor_copy(lg[:, :, :].rearrange("p t e -> p (t e)"), pP[:, 0:TPB * (E + 1)])\
                    .then_inc(lg_ready, 1)
                dve.wait_ge(lg_ready, b + 1)
                for t in range(TPB):
                    step(V.max(top[:, t], lg[:, t, 0:E]))
                settle()
                step(V.tensor_scalar(lm[:, :, E], lg[:, :, E], -1.0, None, ALU.mult))
                V.tensor_tensor(lm[:, :, 0:E], lg[:, :, 0:E], over(top[:, :, 0], E), ALU.subtract)\
                    .then_inc(lm_ready, 1)
                for t in range(TPB):
                    step(V.max_index(tix[:, t], top[:, t], lg[:, t, 0:E]))
                settle()
                it = iota.rearrange("p (o e) -> p o e", o=1).to_broadcast([P, TPB, E])
                step(V.tensor_tensor(eq1[:, :, :], it, over(tix[:, :, 0], E), ALU.is_equal))
                step(V.tensor_tensor(eq2[:, :, :], it, over(tix[:, :, 1], E), ALU.is_equal))
                settle()
                link(V.tensor_tensor(eq1[:, :, :], eq1[:, :, :], eq2[:, :, :], ALU.add))
                dve.wait_ge(ex_ready, b + 1)
                step(V.tensor_reduce(den[:, :, 0], ex[:, :, 0:E], AX.X, ALU.add))
                step(V.tensor_scalar(den[:, :, 1], ex[:, :, E], 1.0, None, ALU.add))
                link(V.tensor_tensor(eq1[:, :, :], eq1[:, :, :], ex[:, :, 0:E], ALU.mult))
                link(V.reciprocal(rden[:, :, :], den[:, :, :]))
                V.tensor_tensor(comb[:, :, 0:E], eq1[:, :, :], over(rden[:, :, 0], E), ALU.mult)
                V.tensor_copy(comb[:, :, E], rden[:, :, 1]).then_inc(comb_ready, 1)

            def comb_pair(b):
                dve.wait_ge(combT_done, b + 1)
                link(V.tensor_copy(cT2[0:E + 1, :], pY[0:E + 1, 0:S]))
                V.tensor_tensor(cT2[32:32 + E + 1, :], pY[0:E + 1, 0:S], cT2[0:E + 1, :], ALU.subtract)\
                    .then_inc(cT_ready, 1)

            def weigh(b, s):
                n = HSESS * b + s
                dve.wait_ge(silu_ready, n + 1)
                dve.wait_ge(cb_done, n + 1)
                if n >= 2:
                    dve.wait_ge(down_done, n - 1)
                if s < HSESS - 1:
                    V.tensor_tensor(hc[:, n % 2].rearrange("p e s -> p (e s)"), pB[:, :],
                                    hh[:, n % 2].rearrange("p e s -> p (e s)"), ALU.mult)\
                        .then_inc(hc_ready, 1)
                else:
                    link(V.tensor_tensor(up[:, :], pH[n % 2][:, S:2 * S], hh[:, n % 2, 0], ALU.mult))
                    V.tensor_tensor(hc[:, n % 2, 0], pB[:, 0:S], up[:, :], ALU.mult).then_inc(hc_ready, 1)

            def finish(b):
                dve.wait_ge(back_done, b + 1)
                if b >= 2:
                    dve.wait_ge(out_done[b % 2], 16 * (b // 2))
                V.tensor_tensor(ob[:, b % 2].rearrange("p t d -> p (t d)"), pY[:, 0:S],
                                x2[:, b % 2].rearrange("p t d -> p (t d)"), ALU.add).then_inc(ob_ready, 1)

            for b in range(B + 1):
                if b < B:
                    scores_decay(b)
                if b >= 1:
                    xn_low(b - 1)
                if b < B:
                    states(b)
                if b >= 1:
                    route(b - 1)
                    comb_pair(b - 1)
                if b < B:
                    gather(b)
                for s in range(HSESS):
                    if b >= 1:
                        weigh(b - 1, s)
                    if b < B:
                        if s == 1:
                            variance(b)
                        if s == 3:
                            group_norm(b)
                        if s == 4:
                            layer_norm(b)
                if b >= 1:
                    finish(b - 1)


def constants():
    c = np.zeros((P, K_COLS), np.float32)
    p = np.arange(P)
    c[:, K_ID:K_ID + P] = np.eye(P)
    c[p, K_BLK + p // HD] = 1
    c[:, K_TRI:K_TRI + C] = np.where(np.arange(C)[None, :] < (p % C)[:, None], NEG, 0)
    c[:, K_IOTA:K_IOTA + E] = np.arange(E)
    c[:, K_ONE] = 1
    c[:, K_EPS] = EPS
    c[:, K_HALF:K_HALF + 16] = -0.5
    sel = np.zeros((64, E + 1, P), np.float16)
    for e in range(E + 1):
        sel[e, e] = 1
        sel[32 + e, e] = 1
    return c, sel


def kernel(**inputs):
    import numpy as _np
    import concourse.bacc as _bacc
    from concourse import mybir as _mybir
    from concourse.bass_utils import run_bass_kernel_spmd as _run

    nc = _bacc.Bacc("TRN2", target_bir_lowering=False, num_devices=1)
    a = {k: _np.ascontiguousarray(v) for k, v in inputs.items()}
    const, sel = constants()
    named = [("x", a["x"]), ("ctx", a["ctx_1024"]), ("wi", a["L0_xattn_Wi_w"]), ("wf", a["L0_xattn_Wf_w"]),
             ("bi", _np.tile(a["L0_xattn_Wi_b"], B).reshape(BH, 1)),
             ("bf", _np.tile(a["L0_xattn_Wf_b"], B).reshape(BH, 1)),
             ("gnw", _np.tile(a["L0_xattn_gn_w"], (P, 1))), ("gnb", _np.tile(a["L0_xattn_gn_b"], (P, 1))),
             ("router", a["L0_ffn_router_w"]), ("gate", a["L0_ffn_shared_gate_w"]), ("w1", a["L0_ffn_w1"]),
             ("w2", a["L0_ffn_w2"]), ("gu", a["L0_ffn_shared_gate_up"]), ("down", a["L0_ffn_shared_down"]),
             ("const", const), ("sel", sel)]
    arrays, args = {}, []
    for name, v in named:
        arrays[f"in_{name}"] = v
        args.append(nc.dram_tensor(f"in_{name}", v.shape, _mybir.dt.from_np(v.dtype),
                                   kind="ExternalInput").ap())
    args.append(nc.dram_tensor("m_scratch", (NC, BH, C), _mybir.dt.float32, kind="Internal").ap())
    args.append(nc.dram_tensor("out_0", (B, S, D), _mybir.dt.float32, kind="ExternalOutput").ap())
    xattn_moe(nc, *args)
    r = _run(nc, [arrays], core_ids=[0])
    return r.results[0]["out_0"]
```

```python
import numpy as np
from contextlib import ExitStack

import concourse.bass as bass
from concourse import mybir

B, S, D = 8, 256, 128
H, HD = 8, 16
E = 8
P = 128
C = 64
NT = B * S // P
TPB = S // P
NC = S // C
VW = HD + 1
HW = H * VW
BH = B * H
GRP = 4
NG = NT // GRP
HB = B // 2
HR = HB * H
EPS = 1e-5
NEG = -1e30

K_ID, K_BLK, K_TRI, K_IOTA, K_ONE, K_EPS, K_HALF = 0, 128, 136, 200, 208, 209, 210
K_MASK = K_HALF + 16
K_COLS = K_MASK + H * VW


def xattn_moe(nc, x_d, ctx_d, wi_d, wf_d, bi_d, bf_d, gnw_d, gnb_d, router_d, gate_d, w1_d, w2_d, gu_d,
              down_d, const_d, sel_d, m_scratch, out_d):
    f32, f16, u32 = mybir.dt.float32, mybir.dt.float16, mybir.dt.uint32
    ALU, ACT, AX = mybir.AluOpType, mybir.ActivationFunctionType, mybir.AxisListType
    ctx = ExitStack()
    with ctx:
        def sb(name, shape, dt=f32):
            return ctx.enter_context(nc.sbuf_tensor(name, shape, dt))

        def sem(name):
            return ctx.enter_context(nc.semaphore(name))

        const = sb("const", [P, K_COLS])
        sel = sb("sel", [64, E + 1, P], f16)
        xs = sb("xs", [P, NT, D])
        cx = sb("cx", [P, NT, D])
        q = sb("q", [P, NT, D])
        qT = sb("qT", [P, B * S])
        qT2 = sb("qT2", [P, 2, B * S], f16)
        kT2 = sb("kT2", [P, 2, B * S], f16)
        v2 = sb("v2", [P, 2, NT, H, VW], f16)
        wg = sb("wg", [2 * H, 3 * D])
        wgT = sb("wgT", [P, 3, 2 * H])
        wgs = sb("wgs", [P, 2, 2 * H])
        wg2 = sb("wg2", [P, 2, 2, 2 * H], f16)
        bi = sb("bi", [BH, 1])
        bf = sb("bf", [BH, 1])
        gnw = sb("gnw", [P, D])
        gnb = sb("gnb", [P, D])
        w1 = sb("w1", [P, E + 2, D])
        w12 = sb("w12", [P, 2, E + 2, D], f16)
        w2 = sb("w2", [P, E + 1, D])
        wr = sb("wr", [P, E + 1])
        wr2 = sb("wr2", [P, 2, E + 1], f16)
        st1 = sb("st1", [P, NT, 6])
        mv1 = sb("mv1", [P, NT, 2])
        ve1 = sb("ve1", [P, NT])
        rs1 = sb("rs1", [P, NT])
        gtok = sb("gtok", [P, 2, TPB, B, H])
        absf = sb("absf", [BH, S])
        ef = sb("ef", [BH, S])
        lf = sb("lf", [BH, S])
        mf = sb("mf", [BH, S])
        csum = sb("csum", [BH, S])
        gg = sb("gg", [BH, S])
        mm = sb("mm", [BH, S])
        md = sb("md", [BH, S])
        negR = sb("negR", [BH, NC])
        em = sb("em", [BH, S])
        wq = sb("wq", [BH, S])
        wk = sb("wk", [BH, NC - 1, S])
        tok = sb("tok", [P, 10, B, H])
        T_G, T_EM, T_WQ, T_WK = 0, 2, 4, 6
        qblk = sb("qblk", [P, 2, 2, H, S], f16)
        mb = sb("mb", [P, 2, TPB, H, C])
        dd = sb("dd", [P, 2, TPB, H, C])
        ct = sb("ct", [P, 2, TPB, H, C])
        ct2 = sb("ct2", [P, 2, 2, TPB, H, C], f16)
        kw = sb("kw", [P, 2, 4, H, VW])
        cst = sb("cst", [P, 2, NC - 1, H, VW])
        ti = sb("ti", [P, TPB, H, VW])
        y = sb("y", [P, TPB, H, VW])
        ssum = sb("ssum", [P, TPB * H])
        rr = sb("rr", [P, TPB * H])
        r2 = sb("r2", [P, TPB * H])
        mean = sb("mean", [P, TPB * H])
        yc = sb("yc", [P, TPB * H, HD])
        sq = sb("sq", [P, TPB * H, HD])
        vs = sb("vs", [P, TPB * H])
        ve = sb("ve", [P, TPB * H])
        rstd = sb("rstd", [P, TPB * H])
        fac = sb("fac", [P, TPB * H])
        yn = sb("yn", [P, TPB, D])
        yw = sb("yw", [P, TPB, D])
        xg = sb("xg", [P, 2, TPB, D])
        x2 = sb("x2", [P, 2, TPB, D])
        st2 = sb("st2", [P, TPB, 6])
        mv2 = sb("mv2", [P, TPB, 2])
        ve2 = sb("ve2", [P, TPB])
        rs2 = sb("rs2", [P, TPB])
        xn = sb("xn", [P, TPB, D])
        xnT2 = sb("xnT2", [P, 2, S], f16)
        lg = sb("lg", [P, TPB, E + 1])
        top = sb("top", [P, TPB, 8])
        tix = sb("tix", [P, TPB, 8], u32)
        lm = sb("lm", [P, TPB, E + 1])
        ex = sb("ex", [P, TPB, E + 1])
        eq1 = sb("eq1", [P, TPB, E])
        eq2 = sb("eq2", [P, TPB, E])
        den = sb("den", [P, TPB, 2])
        rden = sb("rden", [P, TPB, 2])
        comb = sb("comb", [P, TPB, E + 1])
        cT2 = sb("cT2", [64, S], f16)
        hh = sb("hh", [P, 2, 2, S])
        up = sb("up", [P, S])
        hc = sb("hc", [P, 2, 2, S])
        yT = sb("yT", [P, S])
        ob = sb("ob", [P, 2, TPB, D])

        ident = const[:, K_ID:K_ID + P]
        blk8 = const[:, K_BLK:K_BLK + H]
        tri = const[:, K_TRI:K_TRI + C]
        iota = const[:, K_IOTA:K_IOTA + E]
        mask = const[:, K_MASK:K_MASK + HW]
        one = const[:, K_ONE:K_ONE + 1]
        neghalf = const[:, K_HALF:K_HALF + 16]

        bank = [ctx.enter_context(nc.psum_tensor(f"bank{i}", [P, 512], f32)) for i in range(8)]
        pS = bank[0:2]
        pP, pC, pY = bank[2], bank[3], bank[4]
        pH = bank[5:7]
        pB = bank[7]

        consts_in, gatew_in, gn_in, ffn_in = sem("consts_in"), sem("gatew_in"), sem("gn_in"), sem("ffn_in")
        x_in = [sem(f"x_in{g}") for g in range(NG)]
        ctx_in = [sem(f"ctx_in{g}") for g in range(NG)]
        m_out, m_in, q_in, out_done = sem("m_out"), [sem("m_in0"), sem("m_in1")], \
            [sem("q_in0"), sem("q_in1")], [sem("out_done0"), sem("out_done1")]
        zeros_set, ones_set = sem("zeros_set"), sem("ones_set")
        var1_ready, rstd1_ready, q_ready = sem("var1_ready"), sem("rstd1_ready"), sem("q_ready")
        qT_done, kT_done, qT_hi, kT_hi, qT_lo, kT_lo = (sem(n) for n in (
            "qT_done", "kT_done", "qT_hi", "kT_hi", "qT_lo", "kT_lo"))
        qT_copied = sem("qT_copied")
        v_hi, v_lo = sem("v_hi"), sem("v_lo")
        wgT_done, wg_split = sem("wgT_done"), sem("wg_split")
        gates_done, gtok_ready, gateT_done = sem("gates_done"), sem("gtok_ready"), sem("gateT_done")
        abs_ready, ln_ready, act_chain = sem("abs_ready"), sem("ln_ready"), sem("act_chain")
        m_ready, negR_ready, md_ready, fac_ready = sem("m_ready"), sem("negR_ready"), sem("md_ready"), \
            sem("fac_ready")
        tokT_done, tok_ready = sem("tokT_done"), sem("tok_ready")
        w1_hi, w1_lo = sem("w1_hi"), sem("w1_lo")
        dve_chain, pool_chain = sem("dve_chain"), sem("pool_chain")
        expo0_ready = sem("expo0_ready")
        kw_ready, expo_ready, decay_ready, xg_ready = sem("kw_ready"), sem("expo_ready"), \
            sem("decay_ready"), sem("xg_ready")
        scores_done, ct_ready, ct_hi, ct_lo = sem("scores_done"), sem("ct_ready"), sem("ct_hi"), sem("ct_lo")
        state_done, cst_ready, intra_done, inter_done, y_ready = sem("state_done"), sem("cst_ready"), \
            sem("intra_done"), sem("inter_done"), sem("y_ready")
        yc_ready, sq_ready, ve_ready, rstd_ready = sem("yc_ready"), sem("sq_ready"), sem("ve_ready"), \
            sem("rstd_ready")
        x2_ready, ve2_ready, rs2_ready, xn_ready = sem("x2_ready"), sem("ve2_ready"), sem("rs2_ready"), \
            sem("xn_ready")
        xnT_done, xnT_hi, xnT_lo = sem("xnT_done"), sem("xnT_hi"), sem("xnT_lo")
        logits_done, lg_ready, lm_ready, ex_ready, comb_ready = sem("logits_done"), sem("lg_ready"), \
            sem("lm_ready"), sem("ex_ready"), sem("comb_ready")
        combT_done, cT_ready = sem("combT_done"), sem("cT_ready")
        hid_done, cb_done, silu_ready, hc_ready, down_done = sem("hid_done"), sem("cb_done"), \
            sem("silu_ready"), sem("hc_ready"), sem("down_done")
        yT_ready, back_done, ob_ready = sem("yT_ready"), sem("back_done"), \
            sem("ob_ready")

        x_v = x_d.rearrange("b (t p) d -> p (b t) d", p=P)
        c_v = ctx_d.rearrange("b (t p) d -> p (b t) d", p=P)
        o_v = out_d.rearrange("b (t p) d -> p (b t) d", p=P)
        HSESS = E // 2 + 1
        block = ctx.enter_context(nc.Block())

        def store(sp, b):
            sp.wait_ge(ob_ready, b + 1)
            sp.dma_start(o_v[:, b * TPB:(b + 1) * TPB, :], ob[:, b % 2]).then_inc(out_done[b % 2], 16)

        def normalise(dve, g):
            dve.wait_ge(rstd1_ready, g + 1)
            for t in range(g * GRP, (g + 1) * GRP):
                ins = nc.vector.tensor_scalar(q[:, t], xs[:, t], mv1[:, t, 0:1], rs1[:, t:t + 1],
                                              ALU.subtract, ALU.mult)
            ins.then_inc(q_ready, 1)

        def mask_tile(eng, b, t):
            return eng.tensor_tensor(
                dd[:, b % 2, t], tri.rearrange("p (o i) -> p o i", o=1).to_broadcast([P, H, C]),
                tok[:, T_G + t, b, :].rearrange("p (h o) -> p h o", o=1).to_broadcast([P, H, C]), ALU.add)

        def minus_m(eng, k, ts):
            ddf = dd[:, k, ts].rearrange("p t h i -> p (t h i)")
            return eng.tensor_tensor(ddf, ddf, mb[:, k, ts].rearrange("p t h i -> p (t h i)"), ALU.subtract)

        def ct_low(eng, k):
            return eng.tensor_tensor(
                ct2[:, k, 1].rearrange("p t h i -> p (t h i)"), ct[:, k].rearrange("p t h i -> p (t h i)"),
                ct2[:, k, 0].rearrange("p t h i -> p (t h i)"), ALU.subtract)

        QBANK = (bank[0], bank[1], bank[3], bank[5])
        CBANK = (bank[2], bank[3], bank[2], bank[6])

        @block.sync
        def _(sp):
            def tiles(g):
                a = g * GRP
                sp.dma_start(xs[:, a:a + GRP, :], x_v[:, a:a + GRP, :]).then_inc(x_in[g], 16)
                sp.dma_start(cx[:, a:a + GRP, :], c_v[:, a:a + GRP, :]).then_inc(ctx_in[g], 16)

            tiles(0)
            sp.dma_start(const[:, :], const_d).then_inc(consts_in, 16)
            tiles(1)
            sp.dma_start(wg[0:H, :], wi_d).then_inc(gatew_in, 16)
            sp.dma_start(wg[H:2 * H, :], wf_d).then_inc(gatew_in, 16)
            sp.dma_start(bi[:, :], bi_d).then_inc(gatew_in, 16)
            sp.dma_start(bf[:, :], bf_d).then_inc(gatew_in, 16)
            tiles(2)
            tiles(3)
            sp.dma_start(gnw[:, :], gnw_d).then_inc(gn_in, 16)
            sp.dma_start(gnb[:, :], gnb_d).then_inc(gn_in, 16)
            sp.dma_start(w1[:, 0:E, :], w1_d.rearrange("e d f -> d e f")).then_inc(ffn_in, 16)
            sp.dma_start(w1[:, E:E + 2, :], gu_d.rearrange("d (g f) -> d g f", g=2)).then_inc(ffn_in, 16)
            sp.dma_start(w2[:, 0:E, :], w2_d.rearrange("e f d -> f e d")).then_inc(ffn_in, 16)
            sp.dma_start(w2[:, E, :], down_d).then_inc(ffn_in, 16)
            sp.dma_start(wr[:, 0:E], router_d).then_inc(ffn_in, 16)
            sp.dma_start(wr[:, E:E + 1], gate_d).then_inc(ffn_in, 16)
            sp.dma_start(sel[:, :, :], sel_d).then_inc(ffn_in, 16)

            def q_planes(b):
                g = b * TPB // GRP
                sp.wait_ge(zeros_set, 2)
                sp.wait_ge(qT_hi, g + 1)
                sp.wait_ge(qT_lo, g + 1)
                if b >= 2:
                    sp.wait_ge(scores_done, TPB * (b - 1))
                for h in range(H):
                    r = slice(h * HD, (h + 1) * HD)
                    sp.dma_start(qblk[r, b % 2, :, h, :], qT2[r, :, b * S:(b + 1) * S])\
                        .then_inc(q_in[b % 2], 16)

            def m_rows(b):
                if b >= 2:
                    sp.wait_ge(decay_ready, b - 1)
                for half in range(2):
                    src = m_scratch[half::2, b * H:(b + 1) * H, :].rearrange("(o t) h i -> o t (h i)", o=1)\
                        .to_broadcast([C, TPB, H * C])
                    sp.dma_start(mb[half * C:(half + 1) * C, b % 2].rearrange("p t h i -> p t (h i)"),
                                 src).then_inc(m_in[b % 2], 16)

            def m_copy(hf):
                r = slice(hf * HR, (hf + 1) * HR)
                sp.wait_ge(m_ready, hf + 1)
                sp.dma_start(m_scratch[:, r, :].rearrange("n r i -> r n i"),
                             mm[r, :].rearrange("r (n i) -> r n i", n=NC)).then_inc(m_out, 16)

            q_planes(0)
            m_copy(0)
            sp.wait_ge(m_out, 16)
            m_rows(0)
            m_rows(1)
            q_planes(1)
            for b in range(B):
                if b == 1:
                    m_copy(1)
                if b + 2 < B:
                    q_planes(b + 2)
                    if b + 2 == HB:
                        sp.wait_ge(m_out, 32)
                    m_rows(b + 2)
                if b >= 2:
                    store(sp, b - 2)
            for b in range(B - 2, B):
                store(sp, b)
            for k in range(2):
                sp.wait_ge(out_done[k], 16 * (B // 2))

        @block.gpsimd
        def _(pool):
            G = nc.gpsimd
            G.memset(v2[:, 0, :, :, HD:VW], 1.0).then_inc(ones_set, 1)
            G.memset(v2[:, 1, :, :, HD:VW], 0.0).then_inc(ones_set, 1)
            G.memset(wk[:, :, :], 0.0).then_inc(ones_set, 1)
            G.memset(wq[:, 0:C], 0.0).then_inc(ones_set, 1)
            G.memset(ti[0:C, 0, :, :], 0.0).then_inc(ones_set, 1)
            G.memset(cT2[:, :], 0.0).then_inc(ones_set, 1)
            G.memset(qblk[:, 1].rearrange("p a h s -> p (a h s)").bitcast(f32), 0.0).then_inc(zeros_set, 1)
            pool.wait_ge(consts_in, 16)

            def inverse_root(g):
                pool.wait_ge(var1_ready, g + 1)
                s = slice(g * GRP, (g + 1) * GRP)
                G.tensor_tensor(rs1[:, s], ve1[:, s], neghalf[:, 0:GRP], ALU.pow).then_inc(rstd1_ready, 1)

            def values_low(g):
                pool.wait_ge(v_hi, g + 1)
                a = slice(g * GRP, (g + 1) * GRP)
                G.tensor_tensor(v2[:, 1, a, :, 0:HD], cx[:, a].rearrange("p t (h d) -> p t h d", h=H),
                                v2[:, 0, a, :, 0:HD], ALU.subtract).then_inc(v_lo, 1)

            def masked_g(b):
                if b >= 2:
                    pool.wait_ge(ct_ready, TPB * (b - 1))
                if b == HB:
                    pool.wait_ge(tok_ready, 2)
                for t in range(TPB if b >= 1 else 1):
                    ins = mask_tile(G, b, t)
                ins.then_inc(pool_chain, 1)

            def exponent(b):
                k = b % 2
                pool.wait_ge(pool_chain, b + 1)
                pool.wait_ge(m_in[k], 32 * (b // 2 + 1))
                minus_m(G, k, slice(0, TPB if b >= 1 else 1)).then_inc(expo_ready, 1)

            def weighted_values(b):
                k = b % 2
                if b >= 2:
                    pool.wait_ge(state_done, b - 1)
                for v in range(4):
                    a = b * TPB + (1 if v == 3 else 0)
                    G.tensor_tensor(
                        kw[:, k, v, :, 0:HD], cx[:, a].rearrange("p (h d) -> p h d", h=H),
                        tok[:, T_WK + v, b, :].rearrange("p (h o) -> p h o", o=1).to_broadcast([P, H, HD]),
                        ALU.mult)
                G.tensor_copy(kw[:, k, :, :, HD], tok[:, T_WK:T_WK + 4, b, :]).then_inc(kw_ready, 1)

            def residual_bias(b):
                if b >= 2:
                    pool.wait_ge(x2_ready, b - 1)
                for t in range(TPB):
                    ins = G.tensor_tensor(xg[:, b % 2, t], xs[:, b * TPB + t], gnb[:, :], ALU.add)
                ins.then_inc(xg_ready, 1)

            def low_half(b):
                k = b % 2
                pool.wait_ge(ct_hi, b + 1)
                if b >= 2:
                    pool.wait_ge(intra_done, TPB * (b - 1))
                ct_low(G, k).then_inc(ct_lo, 1)

            inverse_root(0)
            inverse_root(1)
            inverse_root(2)
            values_low(0)
            inverse_root(3)
            pool.wait_ge(tok_ready, 1)
            masked_g(0)
            exponent(0)
            weighted_values(0)
            masked_g(1)
            exponent(1)
            weighted_values(1)
            pool.wait_ge(gn_in, 32)
            residual_bias(0)
            pool.wait_ge(w1_hi, 1)
            G.tensor_tensor(w12[:, 1], w1[:, :, :], w12[:, 0], ALU.subtract).then_inc(w1_lo, 1)
            for b in range(B):
                if b + 2 < B:
                    masked_g(b + 2)
                    exponent(b + 2)
                    weighted_values(b + 2)
                if b + 1 < B:
                    residual_bias(b + 1)
                pool.wait_ge(ve_ready, b + 1)
                G.tensor_tensor(rstd[:, :], ve[:, :], neghalf, ALU.pow).then_inc(rstd_ready, 1)
                if b + 1 < B:
                    low_half(b + 1)
                if b % 2 == 0 and b // 2 + 1 < NG:
                    values_low(b // 2 + 1)
                pool.wait_ge(ve2_ready, b + 1)
                G.tensor_tensor(rs2[:, :], ve2[:, :], neghalf[:, 0:TPB], ALU.pow).then_inc(rs2_ready, 1)

        @block.scalar
        def _(act):
            A = nc.scalar
            A.preload_act_table_set("natural_log_exp_and_others")

            def values_high(g):
                act.wait_ge(ctx_in[g], 16)
                a = slice(g * GRP, (g + 1) * GRP)
                A.copy(v2[:, 0, a, :, 0:HD], cx[:, a].rearrange("p t (h d) -> p t h d", h=H)).then_inc(v_hi, 1)

            def ctx_high(g):
                s = slice(g * GRP * P, (g + 1) * GRP * P)
                act.wait_ge(kT_done, g + 1)
                A.copy(kT2[:, 0, s], CBANK[g][:, :]).then_inc(kT_hi, 1)

            def q_high(g):
                s = slice(g * GRP * P, (g + 1) * GRP * P)
                act.wait_ge(qT_done, g + 1)
                A.copy(qT2[:, 0, s], QBANK[g][:, :]).then_inc(qT_hi, 1)
                A.copy(qT[:, s], QBANK[g][:, :]).then_inc(qT_copied, 1)

            def softplus(hf):
                r = slice(hf * HR, (hf + 1) * HR)
                act.wait_ge(gatew_in, 64)
                act.wait_ge(gateT_done, hf + 1)
                A.activation(absf[r, :], bank[6][r, S:2 * S], ACT.Abs, bias=bf[r, :]).then_inc(abs_ready, 1)
                act.wait_ge(abs_ready, hf + 1)
                A.activation(ef[r, :], absf[r, :], ACT.Exp, scale=-1.0).then_inc(act_chain, 1)
                act.wait_ge(act_chain, hf + 1)
                A.activation(lf[r, :], ef[r, :], ACT.Ln, bias=one[r, :]).then_inc(ln_ready, 1)

            def factors(hf):
                r = slice(hf * HR, (hf + 1) * HR)
                act.wait_ge(negR_ready, hf + 1)
                for n in range(NC - 1):
                    A.activation(wk[r, n, 0:(n + 1) * C], gg[r, 0:(n + 1) * C], ACT.Exp,
                                 bias=negR[r, n:n + 1])
                    A.activation(wq[r, (n + 1) * C:(n + 2) * C], mm[r, (n + 1) * C:(n + 2) * C],
                                 ACT.Exp, bias=mm[r, (n + 1) * C - 1:(n + 1) * C], scale=-1.0)
                act.wait_ge(md_ready, hf + 1)
                A.activation(em[r, :], md[r, :], ACT.Exp, scale=-1.0).then_inc(fac_ready, 1)

            def decay(b):
                act.wait_ge(expo_ready, b + 1)
                if b == 0:
                    act.wait_ge(expo0_ready, 1)
                f = dd[:, b % 2].rearrange("p t h i -> p (t h i)")
                A.activation(f, f, ACT.Exp).then_inc(decay_ready, 1)

            def ct_high(b):
                k = b % 2
                act.wait_ge(ct_ready, TPB * (b + 1))
                if b >= 2:
                    act.wait_ge(intra_done, TPB * (b - 1))
                A.copy(ct2[:, k, 0].rearrange("p t h i -> p (t h i)"),
                       ct[:, k].rearrange("p t h i -> p (t h i)")).then_inc(ct_hi, 1)

            def xn_high(b):
                act.wait_ge(xnT_done, b + 1)
                A.copy(xnT2[:, 0], pB[:, 0:S]).then_inc(xnT_hi, 1)

            def router_exp(b):
                act.wait_ge(lm_ready, b + 1)
                A.activation(ex[:, :, :], lm[:, :, :], ACT.Exp).then_inc(ex_ready, 1)

            def silu(b, s):
                n = HSESS * b + s
                act.wait_ge(hid_done, n + 1)
                if n >= 2:
                    act.wait_ge(hc_ready, n - 1)
                w = 2 * S if s < HSESS - 1 else S
                A.activation(hh[:, n % 2].rearrange("p e s -> p (e s)")[:, 0:w], pH[n % 2][:, 0:w],
                             ACT.Silu).then_inc(silu_ready, 1)

            ctx_high(0)
            q_high(0)
            ctx_high(1)
            q_high(1)
            act.wait_ge(ones_set, 6)
            values_high(0)
            ctx_high(2)
            softplus(0)
            q_high(2)
            factors(0)
            act.wait_ge(ffn_in, 16 * 7)
            A.copy(w12[:, 0], w1[:, :, :]).then_inc(w1_hi, 1)
            ctx_high(3)
            q_high(3)
            decay(0)
            ct_high(0)
            softplus(1)
            for b in range(B + 1):
                if b >= 1:
                    xn_high(b - 1)
                if b + 1 < B:
                    decay(b + 1)
                if b >= 1:
                    router_exp(b - 1)
                    A.preload_act_table_set("silu_and_others")
                    silu(b - 1, 0)
                    silu(b - 1, 1)
                if b < B:
                    act.wait_ge(yc_ready, b + 1)
                    A.activation(sq[:, :, :], yc[:, :, :], ACT.Square).then_inc(sq_ready, 1)
                if b == 0:
                    factors(1)
                if b + 1 < B:
                    ct_high(b + 1)
                if b >= 1:
                    silu(b - 1, 2)
                if b % 2 == 0 and b // 2 + 1 < NG:
                    values_high(b // 2 + 1)
                if b >= 1:
                    for s in range(3, HSESS):
                        silu(b - 1, s)
                    act.wait_ge(down_done, HSESS * b)
                    A.copy(yT[:, :], pY[:, 0:S]).then_inc(yT_ready, 1)
                if 1 <= b < B:
                    A.preload_act_table_set("natural_log_exp_and_others")

        @block.tensor
        def _(pe):
            PAIR = ((0, 0), (1, 0), (0, 1))

            pe.wait_ge(consts_in, 16)

            def turn_ctx(g):
                pe.wait_ge(ctx_in[g], 16)
                for t in range(GRP):
                    ins = pe.transpose(CBANK[g][:, t * P:(t + 1) * P], cx[:, g * GRP + t], ident)
                ins.then_inc(kT_done, 1)

            def turn_q(g):
                pe.wait_ge(q_ready, g + 1)
                for t in range(GRP):
                    ins = pe.transpose(QBANK[g][:, t * P:(t + 1) * P], q[:, g * GRP + t, :], ident)
                ins.then_inc(qT_done, 1)

            def gates(g):
                pe.wait_ge(qT_lo, g + 1)
                pe.wait_ge(kT_lo, g + 1)
                for t in range(g * GRP, (g + 1) * GRP):
                    o = bank[4][:, t * 16:(t + 1) * 16]
                    s = slice(t * P, (t + 1) * P)
                    for j, src in enumerate((qT2, kT2)):
                        for i, (u, v) in enumerate(PAIR):
                            ins = pe.matmul(o, src[:, u, s], wg2[:, v, j],
                                            start=(i + j == 0), stop=(i == 2 and j == 1))
                return ins

            def turn_gates(hf):
                n = hf + 1
                pe.wait_ge(gtok_ready, n)
                for i in range(2):
                    for t in range(TPB):
                        ins = pe.transpose(bank[6][0:n * HR, (i * TPB + t) * P:(i * TPB + t + 1) * P],
                                           gtok[:, i, t, 0:n * HB].rearrange("p b h -> p (b h)"), ident)
                ins.then_inc(gateT_done, 1)

            def turn_factors(hf):
                r = slice(hf * HR, (hf + 1) * HR)
                pe.wait_ge(fac_ready, hf + 1)
                pe.wait_ge(md_ready, hf + 1)
                if hf:
                    pe.wait_ge(tok_ready, hf)
                parts = [gg[r, 0:P], gg[r, P:S], em[r, 0:P], em[r, P:S], wq[r, 0:P], wq[r, P:S],
                         wk[r, 0, 0:P], wk[r, 1, 0:P], wk[r, 2, 0:P], wk[r, 2, P:S]]
                for i, part in enumerate(parts):
                    ins = pe.transpose(bank[7][:, i * HR:(i + 1) * HR], part, ident[r, r])
                ins.then_inc(tokT_done, 1)

            def scores(b, t):
                k = b % 2
                pe.wait_ge(q_in[k], 16 * H * (b // 2 + 1))
                if b >= 1:
                    pe.wait_ge(ct_ready, TPB * (b - 1) + t + 1)
                for i, (u, v) in enumerate(PAIR):
                    for half in range(2):
                        n = 2 * t + half
                        a = b * S + n * C
                        ins = pe.matmul(pS[t][half * C:(half + 1) * C, :], kT2[:, u, a:a + C],
                                        qblk[:, k, v, :, n * C:(n + 1) * C],
                                        start=(i == 0), stop=(i == 2))
                ins.then_inc(scores_done, 1)

            def states(b):
                k = b % 2
                pe.wait_ge(kw_ready, b + 1)
                if b >= 1:
                    pe.wait_ge(y_ready, b)
                pe.matmul(pC[:, 0:3 * HW], cx[:, b * TPB], kw[:, k, 0:3].rearrange("p n h v -> p (n h v)"),
                          start=True, stop=False)
                pe.matmul(pC[:, 2 * HW:3 * HW], cx[:, b * TPB + 1], kw[:, k, 3].rearrange("p h v -> p (h v)"),
                          start=False, stop=True).then_inc(state_done, 1)

            def intra(b, t):
                k = b % 2
                if t == 0:
                    pe.wait_ge(ct_lo, b + 1)
                    pe.wait_ge(v_lo, b * TPB // GRP + 1)
                    if b >= 1:
                        pe.wait_ge(y_ready, b)
                for h in range(H):
                    for i, (u, v) in enumerate(PAIR):
                        for half in range(2):
                            r = slice(half * C, (half + 1) * C)
                            ins = pe.matmul(pP[r, t * HW + h * VW:t * HW + (h + 1) * VW],
                                            ct2[r, k, u, t, h, :], v2[r, v, b * TPB + t, h, :],
                                            start=(i == 0), stop=(i == 2))
                ins.then_inc(intra_done, 1)

            def inter(b):
                k = b % 2
                pe.wait_ge(cst_ready, b + 1)
                for n in range(1, NC):
                    t, half = n // 2, n % 2
                    a = b * S + n * C
                    ins = pe.matmul(pC[half * C:(half + 1) * C, t * HW:(t + 1) * HW], qT[:, a:a + C],
                                    cst[:, k, n - 1].rearrange("p h v -> p (h v)"), start=True, stop=True)
                ins.then_inc(inter_done, 1)

            def xn_turn(b):
                pe.wait_ge(xn_ready, b + 1)
                if b >= 1:
                    pe.wait_ge(hc_ready, HSESS * b)
                for t in range(TPB):
                    ins = pe.transpose(pB[:, t * P:(t + 1) * P], xn[:, t], ident)
                ins.then_inc(xnT_done, 1)

            def logits(b):
                pe.wait_ge(xnT_lo, b + 1)
                for t in range(TPB):
                    s = slice(t * P, (t + 1) * P)
                    for i, (u, v) in enumerate(PAIR):
                        ins = pe.matmul(pB[:, S + t * (E + 1):S + (t + 1) * (E + 1)], xnT2[:, u, s], wr2[:, v],
                                        start=(i == 0), stop=(i == 2))
                ins.then_inc(logits_done, 1)

            def comb_turn(b):
                pe.wait_ge(comb_ready, b + 1)
                for t in range(TPB):
                    ins = pe.transpose(pB[0:E + 1, S + t * P:S + (t + 1) * P], comb[:, t], ident)
                ins.then_inc(combT_done, 1)

            def hidden(b, s):
                n = HSESS * b + s
                if n >= 2:
                    pe.wait_ge(silu_ready, n - 1)
                    if (n - 2) % HSESS == HSESS - 1:
                        pe.wait_ge(hc_ready, n - 1)
                for j in range(2):
                    for i, (u, v) in enumerate(PAIR):
                        ins = pe.matmul(pH[n % 2][:, j * S:(j + 1) * S], w12[:, u, 2 * s + j], xnT2[:, v],
                                        start=(i == 0), stop=(i == 2))
                ins.then_inc(hid_done, 1)

            def weights(b, s):
                n = HSESS * b + s
                if s == 0:
                    pe.wait_ge(cT_ready, b + 1)
                else:
                    pe.wait_ge(hc_ready, n)
                for j in range(2 if s < HSESS - 1 else 1):
                    ins = pe.matmul(pB[:, j * S:(j + 1) * S], sel[:, 2 * s + j], cT2[:, :],
                                    start=True, stop=True)
                ins.then_inc(cb_done, 1)

            def down(b, s):
                n = HSESS * b + s
                pe.wait_ge(hc_ready, n + 1)
                if s == 0 and b >= 1:
                    pe.wait_ge(ob_ready, b)
                for j in range(2 if s < HSESS - 1 else 1):
                    e = 2 * s + j
                    ins = pe.matmul(pY[:, 0:S], w2[:, e], hc[:, n % 2, j], start=(e == 0), stop=(e == E))
                ins.then_inc(down_done, 1)

            def back(b):
                pe.wait_ge(yT_ready, b + 1)
                for t in range(TPB):
                    ins = pe.transpose(pY[:, t * P:(t + 1) * P], yT[:, t * P:(t + 1) * P], ident)
                ins.then_inc(back_done, 1)

            turn_ctx(0)
            turn_q(0)
            turn_ctx(1)
            pe.wait_ge(gatew_in, 64)
            for i in range(3):
                ins = pe.transpose(bank[5][:, i * 16:(i + 1) * 16], wg[:, i * D:(i + 1) * D],
                                   ident[0:2 * H, 0:2 * H])
            ins.then_inc(wgT_done, 1)
            turn_q(1)
            pe.wait_ge(kT_lo, 1)
            turn_ctx(2)
            pe.wait_ge(wg_split, 1)
            gates(0)
            gates(1).then_inc(gates_done, 1)
            turn_gates(0)
            turn_q(2)
            scores(0, 0)
            scores(0, 1)
            turn_factors(0)
            turn_ctx(3)
            turn_q(3)
            pe.wait_ge(qT_lo, 3)
            states(0)
            gates(2)
            gates(3).then_inc(gates_done, 1)
            turn_gates(1)
            for b in range(B + 1):
                f = b - 1
                ahead = b + 1 < B
                if f >= 0:
                    xn_turn(f)
                if b < B:
                    intra(b, 0)
                if f >= 0:
                    logits(f)
                if f >= 1:
                    back(f - 1)
                if b < B:
                    intra(b, 1)
                    inter(b)
                if b == 0:
                    turn_factors(1)
                if b == 1:
                    pe.wait_ge(w1_lo, 1)
                    pe.wait_ge(tok_ready, 2)
                if f >= 0:
                    hidden(f, 0)
                    comb_turn(f)
                    hidden(f, 1)
                if ahead:
                    scores(b + 1, 0)
                    scores(b + 1, 1)
                if f >= 0:
                    weights(f, 0)
                    hidden(f, 2)
                if ahead:
                    states(b + 1)
                if f >= 0:
                    for s in range(HSESS):
                        if s + 1 < HSESS:
                            weights(f, s + 1)
                        down(f, s)
                        if s + 3 < HSESS:
                            hidden(f, s + 3)
            back(B - 1)

        @block.vector
        def _(dve):
            V = nc.vector
            chain = [0]

            def step(ins):
                chain[0] += 1
                ins.then_inc(dve_chain, 1)

            def settle():
                dve.wait_ge(dve_chain, chain[0])

            def link(ins):
                step(ins)
                settle()

            def over(ap, n):
                m = ap.shape[1]
                return ap.rearrange("p (m o) -> p m o", o=1).to_broadcast([ap.shape[0], m, n])

            def stats(g):
                dve.wait_ge(x_in[g], 16)
                for t in range(g * GRP, (g + 1) * GRP):
                    step(V.bn_stats(st1[:, t], xs[:, t]))
                settle()
                for t in range(g * GRP, (g + 1) * GRP):
                    step(V.bn_aggr(mv1[:, t], st1[:, t]))
                settle()
                s = slice(g * GRP, (g + 1) * GRP)
                V.tensor_scalar(ve1[:, s], mv1[:, s, 1], EPS, None, ALU.add).then_inc(var1_ready, 1)

            def low(g):
                s = slice(g * GRP * P, (g + 1) * GRP * P)
                dve.wait_ge(kT_hi, g + 1)
                V.tensor_tensor(kT2[:, 1, s], CBANK[g][:, :], kT2[:, 0, s], ALU.subtract).then_inc(kT_lo, 1)
                dve.wait_ge(qT_copied, g + 1)
                V.tensor_tensor(qT2[:, 1, s], QBANK[g][:, :], qT2[:, 0, s], ALU.subtract)\
                    .then_inc(qT_lo, 1)

            def gate_tokens(hf):
                dve.wait_ge(gates_done, hf + 1)
                src = bank[4][:, 0:2 * H * NT].rearrange("p (b t g h) -> p b t g h", b=B, t=TPB, g=2)
                bs = slice(hf * HB, (hf + 1) * HB)
                for i in range(2):
                    for t in range(TPB):
                        ins = V.tensor_copy(gtok[:, i, t, bs], src[:, bs, t, i, :])
                ins.then_inc(gtok_ready, 1)

            def gate_rows(hf):
                r = slice(hf * HR, (hf + 1) * HR)
                gi, gf = bank[6][r, 0:S], bank[6][r, S:2 * S]
                dve.wait_ge(abs_ready, hf + 1)
                dve.wait_ge(gatew_in, 64)
                link(V.tensor_scalar(mf[r, :], gf, bf[r, :], 0.0, ALU.add, ALU.min))
                dve.wait_ge(ln_ready, hf + 1)
                link(V.tensor_tensor_scan(csum[r, :], mf[r, :], lf[r, :], 0.0, ALU.add, ALU.subtract))
                link(V.scalar_tensor_tensor(gg[r, :], gi, bi[r, :], csum[r, :], ALU.add, ALU.subtract))
                V.tensor_tensor_scan(mm[r, :], gg[r, :], gg[r, :], -3e38, ALU.max, ALU.max)\
                    .then_inc(m_ready, 1)
                dve.wait_ge(m_ready, hf + 1)
                V.tensor_scalar(negR[r, :], mm[r, C - 1::C], -1.0, None, ALU.mult).then_inc(negR_ready, 1)
                V.tensor_tensor(md[r, :], csum[r, :], mm[r, :], ALU.add).then_inc(md_ready, 1)

            def token_factors(hf):
                dve.wait_ge(tokT_done, hf + 1)
                V.tensor_copy(tok[:, :, hf * HB:(hf + 1) * HB].rearrange("p i b h -> p i (b h)"),
                              bank[7][:, 0:10 * HR].rearrange("p (i r) -> p i r", i=10)).then_inc(tok_ready, 1)
                dve.wait_ge(tok_ready, hf + 1)

            V.memset(qblk[:, 0].rearrange("p a h s -> p (a h s)").bitcast(f32), 0.0).then_inc(zeros_set, 1)
            stats(0)
            stats(1)
            normalise(dve, 0)
            normalise(dve, 1)
            low(0)
            dve.wait_ge(wgT_done, 1)
            link(V.tensor_copy(wgT[:, :, :].rearrange("p i g -> p (i g)"), bank[5][:, 0:48]))
            step(V.tensor_copy(wgs[:, 0], wgT[:, 0]))
            link(V.tensor_tensor(wgs[:, 1], wgT[:, 1], wgT[:, 2], ALU.add))
            link(V.tensor_copy(wg2[:, 0], wgs[:, :, :]))
            V.tensor_tensor(wg2[:, 1], wgs[:, :, :], wg2[:, 0], ALU.subtract).then_inc(wg_split, 1)
            low(1)
            stats(2)
            gate_tokens(0)
            normalise(dve, 2)
            gate_rows(0)
            low(2)
            stats(3)
            normalise(dve, 3)
            token_factors(0)
            link(mask_tile(V, 0, 1))
            dve.wait_ge(m_in[0], 32)
            minus_m(V, 0, slice(1, 2)).then_inc(expo0_ready, 1)
            low(3)
            gate_tokens(1)
            dve.wait_ge(ffn_in, 16 * 7)
            link(V.tensor_copy(wr2[:, 0], wr[:, :]))
            link(V.tensor_tensor(wr2[:, 1], wr[:, :], wr2[:, 0], ALU.subtract))

            def scores_decay(b):
                k = b % 2
                dve.wait_ge(decay_ready, b + 1)
                if b >= 2:
                    dve.wait_ge(ct_lo, b - 1)
                for t in range(TPB):
                    dve.wait_ge(scores_done, TPB * b + t + 1)
                    V.scalar_tensor_tensor(ct[:, k, t].rearrange("p h i -> p (h i)"), pS[t][:, :],
                                           HD ** -0.5, dd[:, k, t].rearrange("p h i -> p (h i)"),
                                           ALU.mult, ALU.mult).then_inc(ct_ready, 1)

            def states(b):
                dve.wait_ge(state_done, b + 1)
                if b >= 2:
                    dve.wait_ge(inter_done, b - 1)
                V.tensor_tensor(cst[:, b % 2].rearrange("p n h v -> p n (h v)"),
                                pC[:, 0:3 * HW].rearrange("p (n m) -> p n m", n=3),
                                mask.rearrange("p (o m) -> p o m", o=1).to_broadcast([P, 3, HW]),
                                ALU.mult).then_inc(cst_ready, 1)

            def gather(b):
                dve.wait_ge(inter_done, b + 1)
                step(V.tensor_tensor(ti[C:P, 0], pC[C:P, 0:HW].rearrange("p (h v) -> p h v", h=H),
                                     over(tok[C:P, T_WQ, b, :], VW), ALU.mult))
                link(V.tensor_tensor(ti[:, 1], pC[:, HW:2 * HW].rearrange("p (h v) -> p h v", h=H),
                                     over(tok[:, T_WQ + 1, b, :], VW), ALU.mult))
                V.tensor_tensor(y[:, :].rearrange("p t h v -> p (t h v)"), pP[:, 0:2 * HW],
                                ti[:, :].rearrange("p t h v -> p (t h v)"), ALU.add).then_inc(y_ready, 1)
                dve.wait_ge(y_ready, b + 1)
                yv = y[:, :].rearrange("p t h v -> p (t h) v")
                step(V.tensor_reduce(mean[:, :], yv[:, :, 0:HD], AX.X, ALU.add))
                for t in range(TPB):
                    step(V.scalar_tensor_tensor(ssum[:, t * H:(t + 1) * H], y[:, t, :, HD], -1.0,
                                                tok[:, T_EM + t, b, :], ALU.mult, ALU.max))
                settle()
                step(V.tensor_tensor(ssum[:, :].rearrange("p (t h) -> p t h", t=TPB), y[:, :, :, HD],
                                     ssum[:, :].rearrange("p (t h) -> p t h", t=TPB), ALU.max))
                link(V.tensor_scalar(mean[:, :], mean[:, :], 1.0 / HD, None, ALU.mult))
                V.tensor_tensor(yc[:, :, :], yv[:, :, 0:HD], over(mean[:, :], HD), ALU.subtract)\
                    .then_inc(yc_ready, 1)

            def row_sums(b):
                link(V.tensor_scalar(ssum[:, :], ssum[:, :], 1e-6, None, ALU.add))
                link(V.reciprocal(rr[:, :], ssum[:, :]))
                link(V.tensor_tensor(r2[:, :], rr[:, :], rr[:, :], ALU.mult))

            def variance(b):
                dve.wait_ge(sq_ready, b + 1)
                link(V.tensor_reduce(vs[:, :], sq[:, :, :], AX.X, ALU.add))
                link(V.scalar_tensor_tensor(ve[:, :], vs[:, :], 1.0 / HD, r2[:, :], ALU.mult, ALU.mult))
                V.tensor_scalar(ve[:, :], ve[:, :], EPS, None, ALU.add).then_inc(ve_ready, 1)

            def group_norm(b):
                k = b % 2
                dve.wait_ge(rstd_ready, b + 1)
                dve.wait_ge(xg_ready, b + 1)
                dve.wait_ge(yc_ready, b + 1)
                link(V.tensor_tensor(fac[:, :], rstd[:, :], rr[:, :], ALU.mult))
                link(V.tensor_tensor(yn[:, :, :].rearrange("p t (h d) -> p (t h) d", h=H), yc[:, :, :],
                                     over(fac[:, :], HD), ALU.mult))
                link(V.tensor_tensor(yw[:, :, :], yn[:, :, :],
                                     gnw[:, :].rearrange("p (o d) -> p o d", o=1).to_broadcast([P, TPB, D]),
                                     ALU.mult))
                V.tensor_tensor(x2[:, k], yw[:, :, :], xg[:, k], ALU.add).then_inc(x2_ready, 1)
                dve.wait_ge(x2_ready, b + 1)
                for t in range(TPB):
                    step(V.bn_stats(st2[:, t], x2[:, k, t]))
                settle()
                for t in range(TPB):
                    step(V.bn_aggr(mv2[:, t], st2[:, t]))
                settle()
                V.tensor_scalar(ve2[:, :], mv2[:, :, 1], EPS, None, ALU.add).then_inc(ve2_ready, 1)

            def layer_norm(b):
                dve.wait_ge(rs2_ready, b + 1)
                if b >= 1:
                    dve.wait_ge(xnT_done, b)
                for t in range(TPB):
                    ins = V.tensor_scalar(xn[:, t], x2[:, b % 2, t], mv2[:, t, 0:1], rs2[:, t:t + 1],
                                          ALU.subtract, ALU.mult)
                ins.then_inc(xn_ready, 1)

            def xn_low(b):
                dve.wait_ge(xnT_hi, b + 1)
                V.tensor_tensor(xnT2[:, 1], pB[:, 0:S], xnT2[:, 0], ALU.subtract).then_inc(xnT_lo, 1)

            def route(b):
                dve.wait_ge(logits_done, b + 1)
                link(V.tensor_copy(lg[:, :, :].rearrange("p t e -> p (t e)"), pB[:, S:S + TPB * (E + 1)]))
                for t in range(TPB):
                    step(V.max(top[:, t], lg[:, t, 0:E]))
                step(V.tensor_scalar(lm[:, :, E], lg[:, :, E], -1.0, None, ALU.mult))
                settle()
                V.tensor_tensor(lm[:, :, 0:E], lg[:, :, 0:E], over(top[:, :, 0], E), ALU.subtract)\
                    .then_inc(lm_ready, 1)
                for t in range(TPB):
                    step(V.max_index(tix[:, t], top[:, t], lg[:, t, 0:E]))
                settle()
                it = iota.rearrange("p (o e) -> p o e", o=1).to_broadcast([P, TPB, E])
                step(V.tensor_tensor(eq1[:, :, :], it, over(tix[:, :, 0], E), ALU.is_equal))
                link(V.tensor_tensor(eq2[:, :, :], it, over(tix[:, :, 1], E), ALU.is_equal))
                step(V.tensor_tensor(eq1[:, :, :], eq1[:, :, :], eq2[:, :, :], ALU.add))
                dve.wait_ge(ex_ready, b + 1)
                step(V.tensor_reduce(den[:, :, 0], ex[:, :, 0:E], AX.X, ALU.add))
                link(V.tensor_scalar(den[:, :, 1], ex[:, :, E], 1.0, None, ALU.add))
                step(V.tensor_tensor(eq1[:, :, :], eq1[:, :, :], ex[:, :, 0:E], ALU.mult))
                link(V.reciprocal(rden[:, :, :], den[:, :, :]))
                V.tensor_tensor(comb[:, :, 0:E], eq1[:, :, :], over(rden[:, :, 0], E), ALU.mult)
                V.tensor_copy(comb[:, :, E], rden[:, :, 1]).then_inc(comb_ready, 1)

            def comb_pair(b):
                dve.wait_ge(combT_done, b + 1)
                link(V.tensor_copy(cT2[0:E + 1, :], pB[0:E + 1, S:2 * S]))
                V.tensor_tensor(cT2[32:32 + E + 1, :], pB[0:E + 1, S:2 * S], cT2[0:E + 1, :], ALU.subtract)\
                    .then_inc(cT_ready, 1)

            def weigh(b, s):
                n = HSESS * b + s
                dve.wait_ge(silu_ready, n + 1)
                dve.wait_ge(cb_done, n + 1)
                if n >= 2:
                    dve.wait_ge(down_done, n - 1)
                if s < HSESS - 1:
                    V.tensor_tensor(hc[:, n % 2].rearrange("p e s -> p (e s)"), pB[:, :],
                                    hh[:, n % 2].rearrange("p e s -> p (e s)"), ALU.mult)\
                        .then_inc(hc_ready, 1)
                else:
                    link(V.tensor_tensor(up[:, :], pH[n % 2][:, S:2 * S], hh[:, n % 2, 0], ALU.mult))
                    V.tensor_tensor(hc[:, n % 2, 0], pB[:, 0:S], up[:, :], ALU.mult).then_inc(hc_ready, 1)

            def finish(b):
                dve.wait_ge(back_done, b + 1)
                if b >= 2:
                    dve.wait_ge(out_done[b % 2], 16 * (b // 2))
                V.tensor_tensor(ob[:, b % 2].rearrange("p t d -> p (t d)"), pY[:, 0:S],
                                x2[:, b % 2].rearrange("p t d -> p (t d)"), ALU.add).then_inc(ob_ready, 1)

            scores_decay(0)
            dve.wait_ge(ct_hi, 1)
            ct_low(V, 0).then_inc(ct_lo, 1)
            states(0)
            gate_rows(1)
            for b in range(B + 1):
                f = b - 1
                if f >= 0:
                    xn_low(f)
                if f >= 1:
                    finish(f - 1)
                if f >= 0:
                    route(f)
                if b < B:
                    gather(b)
                if f >= 0:
                    comb_pair(f)
                if b < B:
                    row_sums(b)
                    variance(b)
                if b == 0:
                    token_factors(1)
                if b + 1 < B:
                    scores_decay(b + 1)
                if f >= 0:
                    weigh(f, 0)
                if b + 1 < B:
                    states(b + 1)
                if f >= 0:
                    weigh(f, 1)
                if b < B:
                    group_norm(b)
                if f >= 0:
                    weigh(f, 2)
                if b < B:
                    layer_norm(b)
                if f >= 0:
                    weigh(f, 3)
                    weigh(f, 4)
            finish(B - 1)


def constants():
    c = np.zeros((P, K_COLS), np.float32)
    p = np.arange(P)
    c[:, K_ID:K_ID + P] = np.eye(P)
    c[p, K_BLK + p // HD] = 1
    c[:, K_TRI:K_TRI + C] = np.where(np.arange(C)[None, :] < (p % C)[:, None], NEG, 0)
    c[:, K_IOTA:K_IOTA + E] = np.arange(E)
    c[:, K_ONE] = 1
    c[:, K_EPS] = EPS
    c[:, K_HALF:K_HALF + 16] = -0.5
    for h in range(H):
        c[h * HD:(h + 1) * HD, K_MASK + h * VW:K_MASK + (h + 1) * VW] = HD ** -0.5
    sel = np.zeros((64, E + 1, P), np.float16)
    for e in range(E + 1):
        sel[e, e] = 1
        sel[32 + e, e] = 1
    return c, sel


def kernel(**inputs):
    import numpy as _np
    import concourse.bacc as _bacc
    from concourse import mybir as _mybir
    from concourse.bass_utils import run_bass_kernel_spmd as _run

    nc = _bacc.Bacc("TRN2", target_bir_lowering=False, num_devices=1)
    a = {k: _np.ascontiguousarray(v) for k, v in inputs.items()}
    const, sel = constants()
    named = [("x", a["x"]), ("ctx", a["ctx_1024"]), ("wi", a["L0_xattn_Wi_w"]), ("wf", a["L0_xattn_Wf_w"]),
             ("bi", _np.tile(a["L0_xattn_Wi_b"], B).reshape(BH, 1)),
             ("bf", _np.tile(a["L0_xattn_Wf_b"], B).reshape(BH, 1)),
             ("gnw", _np.tile(a["L0_xattn_gn_w"], (P, 1))), ("gnb", _np.tile(a["L0_xattn_gn_b"], (P, 1))),
             ("router", a["L0_ffn_router_w"]), ("gate", a["L0_ffn_shared_gate_w"]), ("w1", a["L0_ffn_w1"]),
             ("w2", a["L0_ffn_w2"]), ("gu", a["L0_ffn_shared_gate_up"]), ("down", a["L0_ffn_shared_down"]),
             ("const", const), ("sel", sel)]
    arrays, args = {}, []
    for name, v in named:
        arrays[f"in_{name}"] = v
        args.append(nc.dram_tensor(f"in_{name}", v.shape, _mybir.dt.from_np(v.dtype),
                                   kind="ExternalInput").ap())
    args.append(nc.dram_tensor("m_scratch", (NC, BH, C), _mybir.dt.float32, kind="Internal").ap())
    args.append(nc.dram_tensor("out_0", (B, S, D), _mybir.dt.float32, kind="ExternalOutput").ap())
    xattn_moe(nc, *args)
    r = _run(nc, [arrays], core_ids=[0])
    return r.results[0]["out_0"]
```

```python
import numpy as np
from contextlib import ExitStack

import concourse.bass as bass
from concourse import mybir

B, S, D = 8, 256, 128
H, HD = 8, 16
E = 8
P = 128
C = 64
NT = B * S // P
TPB = S // P
NC = S // C
VW = HD + 1
HW = H * VW
BH = B * H
GRP = 4
NG = NT // GRP
HB = B // 2
HR = HB * H
EPS = 1e-5
NEG = -1e30

K_ID = 0
K_TRI = K_ID + P
K_IOTA = K_TRI + C
K_ONE = K_IOTA + E
K_HALF = K_ONE + 1
K_MASK = K_HALF + TPB * H
K_COLS = K_MASK + HW


def xattn_moe(nc, x_d, ctx_d, wi_d, wf_d, bi_d, bf_d, gnw_d, gnb_d, router_d, gate_d, w1_d, w2_d, gu_d,
              down_d, const_d, sel_d, m_scratch, out_d):
    f32, f16, u32 = mybir.dt.float32, mybir.dt.float16, mybir.dt.uint32
    ALU, ACT, AX = mybir.AluOpType, mybir.ActivationFunctionType, mybir.AxisListType
    ctx = ExitStack()
    with ctx:
        def sb(name, shape, dt=f32):
            return ctx.enter_context(nc.sbuf_tensor(name, shape, dt))

        def sem(name):
            return ctx.enter_context(nc.semaphore(name))

        const = sb("const", [P, K_COLS])
        sel = sb("sel", [64, E + 1, P], f16)
        xs = sb("xs", [P, NT, D])
        cx = sb("cx", [P, NT, D])
        vsum = sb("vsum", [P, NT * H])
        vc = sb("vc", [P, NT, D])
        q = sb("q", [P, NT, D])
        qT = sb("qT", [P, B * S])
        qT2 = sb("qT2", [P, 2, B * S], f16)
        kT2 = sb("kT2", [P, 2, B * S], f16)
        v2 = sb("v2", [P, 2, NT, H, VW], f16)
        wg = sb("wg", [2 * H, 3 * D])
        wgT = sb("wgT", [P, 3, 2 * H])
        wgs = sb("wgs", [P, 2, 2 * H])
        wg2 = sb("wg2", [P, 2, 2, 2 * H], f16)
        bi = sb("bi", [BH, 1])
        bf = sb("bf", [BH, 1])
        gnw = sb("gnw", [P, D])
        gnb = sb("gnb", [P, D])
        w1 = sb("w1", [P, E + 2, D])
        w12 = sb("w12", [P, 2, E + 2, D], f16)
        w2 = sb("w2", [P, E + 1, D])
        wr = sb("wr", [P, E + 1])
        wr2 = sb("wr2", [P, 2, E + 1], f16)
        st1 = sb("st1", [P, NT, 6])
        mv1 = sb("mv1", [P, NT, 2])
        ve1 = sb("ve1", [P, NT])
        rs1 = sb("rs1", [P, NT])
        gtok = sb("gtok", [P, 2, TPB, B, H])
        absf = sb("absf", [BH, S])
        ef = sb("ef", [BH, S])
        lf = sb("lf", [BH, S])
        mf = sb("mf", [BH, S])
        csum = sb("csum", [BH, S])
        gg = sb("gg", [BH, S])
        mm = sb("mm", [BH, S])
        md = sb("md", [BH, S])
        negR = sb("negR", [BH, NC])
        em = sb("em", [BH, S])
        wq = sb("wq", [BH, S])
        wk = sb("wk", [BH, NC - 1, S])
        tok = sb("tok", [P, 10, B, H])
        T_G, T_EM, T_WQ, T_WK = 0, 2, 4, 6
        qblk = sb("qblk", [P, 2, 2, H, S], f16)
        mb = sb("mb", [P, 2, TPB, H, C])
        dd = sb("dd", [P, 2, TPB, H, C])
        ct = sb("ct", [P, 2, TPB, H, C])
        ct2 = sb("ct2", [P, 2, 2, TPB, H, C], f16)
        kw = sb("kw", [P, 2, 4, H, VW])
        cst = sb("cst", [P, 2, NC - 1, H, VW])
        ti = sb("ti", [P, TPB, H, VW])
        y = sb("y", [P, TPB, H, VW])
        den = sb("den", [P, TPB, H])
        den2 = sb("den2", [P, TPB, H])
        sq = sb("sq", [P, TPB * H, HD])
        vs = sb("vs", [P, TPB * H])
        ve = sb("ve", [P, TPB * H])
        rstd = sb("rstd", [P, TPB * H])
        yw = sb("yw", [P, TPB, D])
        yn = sb("yn", [P, TPB, D])
        xg = sb("xg", [P, 2, TPB, D])
        x2 = sb("x2", [P, 2, TPB, D])
        st2 = sb("st2", [P, TPB, 6])
        mv2 = sb("mv2", [P, TPB, 2])
        ve2 = sb("ve2", [P, TPB])
        rs2 = sb("rs2", [P, TPB])
        xn = sb("xn", [P, TPB, D])
        xnT2 = sb("xnT2", [P, 2, S], f16)
        lg = sb("lg", [P, TPB, E + 1])
        top = sb("top", [P, TPB, 8])
        tix = sb("tix", [P, TPB, 8], u32)
        lm = sb("lm", [P, TPB, E + 1])
        ex = sb("ex", [P, TPB, E + 1])
        eq1 = sb("eq1", [P, TPB, E])
        eq2 = sb("eq2", [P, TPB, E])
        sden = sb("sden", [P, TPB, 2])
        rden = sb("rden", [P, TPB, 2])
        comb = sb("comb", [P, TPB, E + 1])
        cT2 = sb("cT2", [64, S], f16)
        hh = sb("hh", [P, 2, 2, S])
        up = sb("up", [P, S])
        hc = sb("hc", [P, 2, 2, S])
        yT = sb("yT", [P, S])
        ob = sb("ob", [P, 2, TPB, D])

        ident = const[:, K_ID:K_ID + P]
        tri = const[:, K_TRI:K_TRI + C]
        iota = const[:, K_IOTA:K_IOTA + E]
        mask = const[:, K_MASK:K_MASK + HW]
        one = const[:, K_ONE:K_ONE + 1]
        neghalf = const[:, K_HALF:K_HALF + TPB * H]

        bank = [ctx.enter_context(nc.psum_tensor(f"bank{i}", [P, 512], f32)) for i in range(8)]
        pS = bank[0:2]
        pP, pC, pY = bank[2], bank[3], bank[4]
        pH = bank[5:7]
        pB = bank[7]
        pX = pS[1]

        consts_in, gatew_in, gn_in, ffn_in = sem("consts_in"), sem("gatew_in"), sem("gn_in"), sem("ffn_in")
        x_in = [sem(f"x_in{g}") for g in range(NG)]
        ctx_in = [sem(f"ctx_in{g}") for g in range(NG)]
        m_out, m_in, q_in, out_done = sem("m_out"), [sem("m_in0"), sem("m_in1")], \
            [sem("q_in0"), sem("q_in1")], [sem("out_done0"), sem("out_done1")]
        zeros_set, ones_set = sem("zeros_set"), sem("ones_set")
        var1_ready, rstd1_ready, q_ready = sem("var1_ready"), sem("rstd1_ready"), sem("q_ready")
        qT_done, kT_done, qT_hi, kT_hi, qT_lo, kT_lo = (sem(n) for n in (
            "qT_done", "kT_done", "qT_hi", "kT_hi", "qT_lo", "kT_lo"))
        qT_copied = sem("qT_copied")
        v_hi, v_lo = sem("v_hi"), sem("v_lo")
        wgT_done, wg_split = sem("wgT_done"), sem("wg_split")
        gates_done, gtok_ready, gateT_done = sem("gates_done"), sem("gtok_ready"), sem("gateT_done")
        abs_ready, ln_ready, act_chain = sem("abs_ready"), sem("ln_ready"), sem("act_chain")
        m_ready, negR_ready, md_ready, fac_ready = sem("m_ready"), sem("negR_ready"), sem("md_ready"), \
            sem("fac_ready")
        tokT_done, tok_ready = sem("tokT_done"), sem("tok_ready")
        w1_in, w1_hi, w1_lo = sem("w1_in"), sem("w1_hi"), sem("w1_lo")
        dve_chain, pool_chain = sem("dve_chain"), sem("pool_chain")
        expo0_ready = sem("expo0_ready")
        kw_ready, expo_ready, decay_ready, xg_ready = sem("kw_ready"), sem("expo_ready"), \
            sem("decay_ready"), sem("xg_ready")
        scores_done, ct_ready, ct_hi, ct_lo = sem("scores_done"), sem("ct_ready"), sem("ct_hi"), sem("ct_lo")
        state_done, cst_ready, intra_done, inter_done, y_ready = sem("state_done"), sem("cst_ready"), \
            sem("intra_done"), sem("inter_done"), sem("y_ready")
        last_ready = sem("last_ready")
        vc_ready, back_copied, cT_hi = sem("vc_ready"), sem("back_copied"), sem("cT_hi")
        yw_ready, sq_ready, ve_ready, rstd_ready = sem("yw_ready"), sem("sq_ready"), sem("ve_ready"), \
            sem("rstd_ready")
        x2_ready, ve2_ready, rs2_ready, xn_ready = sem("x2_ready"), sem("ve2_ready"), sem("rs2_ready"), \
            sem("xn_ready")
        xnT_done, xnT_hi, xnT_lo = sem("xnT_done"), sem("xnT_hi"), sem("xnT_lo")
        logits_done, lm_ready, ex_ready, comb_ready = sem("logits_done"), sem("lm_ready"), \
            sem("ex_ready"), sem("comb_ready")
        combT_done, cT_ready = sem("combT_done"), sem("cT_ready")
        hid_done, cb_done, silu_ready, hc_ready, down_done = sem("hid_done"), sem("cb_done"), \
            sem("silu_ready"), sem("hc_ready"), sem("down_done")
        yT_ready, back_done, ob_ready = sem("yT_ready"), sem("back_done"), \
            sem("ob_ready")

        x_v = x_d.rearrange("b (t p) d -> p (b t) d", p=P)
        c_v = ctx_d.rearrange("b (t p) d -> p (b t) d", p=P)
        o_v = out_d.rearrange("b (t p) d -> p (b t) d", p=P)
        HSESS = E // 2 + 1
        block = ctx.enter_context(nc.Block())

        def store(sp, b):
            if b < B - 1:
                sp.wait_ge(ob_ready, b + 1)
            else:
                sp.wait_ge(last_ready, 1)
            sp.dma_start(o_v[:, b * TPB:(b + 1) * TPB, :], ob[:, b % 2]).then_inc(out_done[b % 2], 16)

        def normalise(dve, g):
            dve.wait_ge(rstd1_ready, g + 1)
            for t in range(g * GRP, (g + 1) * GRP):
                ins = nc.vector.tensor_scalar(q[:, t], xs[:, t], mv1[:, t, 0:1], rs1[:, t:t + 1],
                                              ALU.subtract, ALU.mult)
            ins.then_inc(q_ready, 1)

        def m_copy(eng, hf):
            r = slice(hf * HR, (hf + 1) * HR)
            eng.wait_ge(m_ready, hf + 1)
            eng.dma_start(m_scratch[:, r, :].rearrange("n r i -> r n i"),
                          mm[r, :].rearrange("r (n i) -> r n i", n=NC)).then_inc(m_out, 16)

        def m_rows(eng, b):
            if b >= 2:
                eng.wait_ge(decay_ready, b - 1)
            for half in range(2):
                src = m_scratch[half::2, b * H:(b + 1) * H, :].rearrange("(o t) h i -> o t (h i)", o=1)\
                    .to_broadcast([C, TPB, H * C])
                eng.dma_start(mb[half * C:(half + 1) * C, b % 2].rearrange("p t h i -> p t (h i)"),
                              src).then_inc(m_in[b % 2], 16)

        def mask_tile(eng, b, t):
            return eng.tensor_tensor(
                dd[:, b % 2, t], tri.rearrange("p (o i) -> p o i", o=1).to_broadcast([P, H, C]),
                tok[:, T_G + t, b, :].rearrange("p (h o) -> p h o", o=1).to_broadcast([P, H, C]), ALU.add)

        def minus_m(eng, k, ts):
            ddf = dd[:, k, ts].rearrange("p t h i -> p (t h i)")
            return eng.tensor_tensor(ddf, ddf, mb[:, k, ts].rearrange("p t h i -> p (t h i)"), ALU.subtract)

        def ct_low(eng, k):
            return eng.tensor_tensor(
                ct2[:, k, 1].rearrange("p t h i -> p (t h i)"), ct[:, k].rearrange("p t h i -> p (t h i)"),
                ct2[:, k, 0].rearrange("p t h i -> p (t h i)"), ALU.subtract)

        QBANK = (bank[0], bank[1], bank[5], bank[5])
        CBANK = (bank[2], bank[3], bank[2], bank[6])

        @block.sync
        def _(sp):
            def tiles(g):
                a = g * GRP
                sp.dma_start(xs[:, a:a + GRP, :], x_v[:, a:a + GRP, :]).then_inc(x_in[g], 16)
                sp.dma_start(cx[:, a:a + GRP, :], c_v[:, a:a + GRP, :]).then_inc(ctx_in[g], 16)

            tiles(0)
            sp.dma_start(const[:, :], const_d).then_inc(consts_in, 16)
            tiles(1)
            sp.dma_start(wg[0:H, :], wi_d).then_inc(gatew_in, 16)
            sp.dma_start(wg[H:2 * H, :], wf_d).then_inc(gatew_in, 16)
            sp.dma_start(bi[:, :], bi_d).then_inc(gatew_in, 16)
            sp.dma_start(bf[:, :], bf_d).then_inc(gatew_in, 16)
            tiles(2)
            tiles(3)
            sp.dma_start(gnw[:, :], gnw_d).then_inc(gn_in, 16)
            sp.dma_start(gnb[:, :], gnb_d).then_inc(gn_in, 16)

            def q_planes(b):
                g = b * TPB // GRP
                sp.wait_ge(zeros_set, 2)
                sp.wait_ge(qT_hi, g + 1)
                sp.wait_ge(qT_lo, g + 1)
                if b >= 2:
                    sp.wait_ge(scores_done, TPB * (b - 1))
                for h in range(H):
                    r = slice(h * HD, (h + 1) * HD)
                    sp.dma_start(qblk[r, b % 2, :, h, :], qT2[r, :, b * S:(b + 1) * S])\
                        .then_inc(q_in[b % 2], 16)

            q_planes(0)
            q_planes(1)
            sp.dma_start(w1[:, 0:E, :], w1_d.rearrange("e d f -> d e f")).then_inc(w1_in, 16)
            sp.dma_start(w1[:, E:E + 2, :], gu_d.rearrange("d (g f) -> d g f", g=2)).then_inc(w1_in, 16)
            sp.dma_start(w2[:, 0:E, :], w2_d.rearrange("e f d -> f e d")).then_inc(ffn_in, 16)
            sp.dma_start(w2[:, E, :], down_d).then_inc(ffn_in, 16)
            sp.dma_start(wr[:, 0:E], router_d).then_inc(ffn_in, 16)
            sp.dma_start(wr[:, E:E + 1], gate_d).then_inc(ffn_in, 16)
            sp.dma_start(sel[:, :, :], sel_d).then_inc(ffn_in, 16)
            for b in range(B):
                if b == 1:
                    m_copy(sp, 1)
                if b + 2 < B:
                    if b + 2 == HB:
                        sp.wait_ge(m_out, 32)
                    m_rows(sp, b + 2)
                    q_planes(b + 2)
                if b >= 2:
                    store(sp, b - 2)
            for b in range(B - 2, B):
                store(sp, b)
            for k in range(2):
                sp.wait_ge(out_done[k], 16 * (B // 2))

        @block.gpsimd
        def _(pool):
            G = nc.gpsimd
            G.memset(v2[:, 0, :, :, HD:VW], 1.0).then_inc(ones_set, 1)
            G.memset(v2[:, 1, :, :, HD:VW], 0.0).then_inc(ones_set, 1)
            G.memset(wk[:, :, :], 0.0).then_inc(ones_set, 1)
            G.memset(wq[:, 0:C], 0.0).then_inc(ones_set, 1)
            G.memset(ti[0:C, 0, :, :], 0.0).then_inc(ones_set, 1)
            G.memset(cT2[:, :], 0.0).then_inc(ones_set, 1)
            G.memset(qblk[:, 1].rearrange("p a h s -> p (a h s)").bitcast(f32), 0.0).then_inc(zeros_set, 1)
            pool.wait_ge(consts_in, 16)

            def inverse_root(g):
                pool.wait_ge(var1_ready, g + 1)
                s = slice(g * GRP, (g + 1) * GRP)
                G.tensor_tensor(rs1[:, s], ve1[:, s], neghalf[:, 0:GRP], ALU.pow).then_inc(rstd1_ready, 1)

            def values_low(g):
                pool.wait_ge(v_hi, g + 1)
                a = slice(g * GRP, (g + 1) * GRP)
                G.tensor_tensor(v2[:, 1, a, :, 0:HD], vc[:, a].rearrange("p t (h d) -> p t h d", h=H),
                                v2[:, 0, a, :, 0:HD], ALU.subtract).then_inc(v_lo, 1)

            def masked_g(b):
                if b >= 2:
                    pool.wait_ge(ct_ready, TPB * (b - 1))
                if b == HB:
                    pool.wait_ge(tok_ready, 2)
                for t in range(TPB if b >= 1 else 1):
                    ins = mask_tile(G, b, t)
                ins.then_inc(pool_chain, 1)

            def exponent(b):
                k = b % 2
                pool.wait_ge(pool_chain, b + 1)
                pool.wait_ge(m_in[k], 32 * (b // 2 + 1))
                minus_m(G, k, slice(0, TPB if b >= 1 else 1)).then_inc(expo_ready, 1)

            def weighted_values(b):
                k = b % 2
                pool.wait_ge(vc_ready, b * TPB // GRP + 1)
                if b >= 2:
                    pool.wait_ge(state_done, b - 1)
                for v in range(4):
                    a = b * TPB + (1 if v == 3 else 0)
                    G.tensor_tensor(
                        kw[:, k, v, :, 0:HD], vc[:, a].rearrange("p (h d) -> p h d", h=H),
                        tok[:, T_WK + v, b, :].rearrange("p (h o) -> p h o", o=1).to_broadcast([P, H, HD]),
                        ALU.mult)
                G.tensor_copy(kw[:, k, :, :, HD], tok[:, T_WK:T_WK + 4, b, :]).then_inc(kw_ready, 1)

            def residual_bias(b):
                if b >= 2:
                    pool.wait_ge(x2_ready, b - 1)
                for t in range(TPB):
                    ins = G.tensor_tensor(xg[:, b % 2, t], xs[:, b * TPB + t], gnb[:, :], ALU.add)
                ins.then_inc(xg_ready, 1)

            def times_weight(b):
                pool.wait_ge(y_ready, b + 1)
                if b >= 1:
                    pool.wait_ge(x2_ready, b)
                G.tensor_tensor(yw[:, :, :].rearrange("p t (h d) -> p t h d", h=H), y[:, :, :, 0:HD],
                                gnw[:, :].rearrange("p (o h d) -> p o h d", o=1, h=H)
                                .to_broadcast([P, TPB, H, HD]), ALU.mult).then_inc(yw_ready, 1)

            def head_root(b):
                pool.wait_ge(ve_ready, b + 1)
                G.tensor_tensor(rstd[:, :], ve[:, :], neghalf, ALU.pow).then_inc(rstd_ready, 1)

            def token_root(b):
                pool.wait_ge(ve2_ready, b + 1)
                G.tensor_tensor(rs2[:, :], ve2[:, :], neghalf[:, 0:TPB], ALU.pow).then_inc(rs2_ready, 1)

            def finish(b):
                pool.wait_ge(back_copied, b + 1)
                G.tensor_tensor(ob[:, b % 2], ob[:, b % 2], x2[:, b % 2], ALU.add).then_inc(ob_ready, 1)

            inverse_root(0)
            inverse_root(1)
            inverse_root(2)
            pool.wait_ge(gn_in, 32)
            residual_bias(0)
            pool.wait_ge(tok_ready, 1)
            masked_g(0)
            weighted_values(0)
            exponent(0)
            inverse_root(3)
            masked_g(1)
            values_low(0)
            exponent(1)
            weighted_values(1)
            pool.wait_ge(w1_hi, 1)
            G.tensor_tensor(w12[:, 1], w1[:, :, :], w12[:, 0], ALU.subtract).then_inc(w1_lo, 1)
            times_weight(0)
            head_root(0)
            residual_bias(1)
            token_root(0)
            masked_g(2)
            exponent(2)
            values_low(1)
            weighted_values(2)
            for b in range(1, B):
                if 1 < b < B - 2:
                    masked_g(b + 2)
                    exponent(b + 2)
                times_weight(b)
                if b + 1 < B:
                    residual_bias(b + 1)
                head_root(b)
                if b == 1:
                    masked_g(b + 2)
                    exponent(b + 2)
                if b >= 2:
                    finish(b - 2)
                if b + 2 < B:
                    weighted_values(b + 2)
                token_root(b)
                if b % 2 == 0 and b // 2 + 1 < NG:
                    values_low(b // 2 + 1)
            finish(B - 2)

        @block.scalar
        def _(act):
            A = nc.scalar
            A.preload_act_table_set("natural_log_exp_and_others")

            def values_high(g):
                act.wait_ge(vc_ready, g + 1)
                a = slice(g * GRP, (g + 1) * GRP)
                A.copy(v2[:, 0, a, :, 0:HD], vc[:, a].rearrange("p t (h d) -> p t h d", h=H))\
                    .then_inc(v_hi, 1)

            def ctx_high(g):
                s = slice(g * GRP * P, (g + 1) * GRP * P)
                act.wait_ge(kT_done, g + 1)
                A.copy(kT2[:, 0, s], CBANK[g][:, :]).then_inc(kT_hi, 1)

            def q_high(g):
                s = slice(g * GRP * P, (g + 1) * GRP * P)
                act.wait_ge(qT_done, g + 1)
                A.copy(qT2[:, 0, s], QBANK[g][:, :]).then_inc(qT_hi, 1)

            def q_copy(g):
                s = slice(g * GRP * P, (g + 1) * GRP * P)
                act.wait_ge(qT_lo, g + 1)
                A.copy(qT[:, s], QBANK[g][:, :]).then_inc(qT_copied, 1)

            def softplus(hf):
                r = slice(hf * HR, (hf + 1) * HR)
                act.wait_ge(gatew_in, 64)
                act.wait_ge(gateT_done, hf + 1)
                A.activation(absf[r, :], bank[6][r, S:2 * S], ACT.Abs, bias=bf[r, :]).then_inc(abs_ready, 1)
                act.wait_ge(abs_ready, hf + 1)
                A.activation(ef[r, :], absf[r, :], ACT.Exp, scale=-1.0).then_inc(act_chain, 1)
                act.wait_ge(act_chain, hf + 1)
                A.activation(lf[r, :], ef[r, :], ACT.Ln, bias=one[r, :]).then_inc(ln_ready, 1)

            def factors(hf):
                r = slice(hf * HR, (hf + 1) * HR)
                act.wait_ge(negR_ready, hf + 1)
                for n in range(NC - 1):
                    A.activation(wk[r, n, 0:(n + 1) * C], gg[r, 0:(n + 1) * C], ACT.Exp,
                                 bias=negR[r, n:n + 1])
                    A.activation(wq[r, (n + 1) * C:(n + 2) * C], mm[r, (n + 1) * C:(n + 2) * C],
                                 ACT.Exp, bias=mm[r, (n + 1) * C - 1:(n + 1) * C], scale=-1.0)
                act.wait_ge(md_ready, hf + 1)
                A.activation(em[r, :], md[r, :], ACT.Exp, scale=-1.0).then_inc(fac_ready, 1)

            def decay(b):
                act.wait_ge(expo_ready, b + 1)
                if b == 0:
                    act.wait_ge(expo0_ready, 1)
                f = dd[:, b % 2].rearrange("p t h i -> p (t h i)")
                A.activation(f, f, ACT.Exp).then_inc(decay_ready, 1)

            def ct_high(b):
                k = b % 2
                act.wait_ge(ct_ready, TPB * (b + 1))
                if b >= 2:
                    act.wait_ge(intra_done, TPB * (b - 1))
                A.copy(ct2[:, k, 0].rearrange("p t h i -> p (t h i)"),
                       ct[:, k].rearrange("p t h i -> p (t h i)")).then_inc(ct_hi, 1)

            def xn_high(b):
                act.wait_ge(xnT_done, b + 1)
                A.copy(xnT2[:, 0], pX[:, 0:S]).then_inc(xnT_hi, 1)

            def router_exp(b):
                act.wait_ge(lm_ready, b + 1)
                A.activation(ex[:, :, :], lm[:, :, :], ACT.Exp).then_inc(ex_ready, 1)

            def silu(b, s):
                n = HSESS * b + s
                act.wait_ge(hid_done, n + 1)
                if n >= 2:
                    act.wait_ge(hc_ready, n - 1)
                w = 2 * S if s < HSESS - 1 else S
                A.activation(hh[:, n % 2].rearrange("p e s -> p (e s)")[:, 0:w], pH[n % 2][:, 0:w],
                             ACT.Silu).then_inc(silu_ready, 1)

            ctx_high(0)
            q_high(0)
            ctx_high(1)
            q_high(1)
            q_copy(0)
            q_copy(1)
            ctx_high(2)
            softplus(0)
            m_copy(act, 0)
            factors(0)
            act.wait_ge(m_out, 16)
            m_rows(act, 0)
            m_rows(act, 1)
            q_high(2)
            ctx_high(3)
            decay(0)
            act.wait_ge(ones_set, 6)
            values_high(0)
            q_copy(2)
            ct_high(0)
            act.wait_ge(w1_in, 32)
            A.copy(w12[:, 0], w1[:, :, :]).then_inc(w1_hi, 1)
            decay(1)
            q_high(3)

            def cT_high(b):
                act.wait_ge(combT_done, b + 1)
                A.copy(cT2[0:E + 1, :], pX[0:E + 1, S:2 * S]).then_inc(cT_hi, 1)

            def experts_sum(b):
                act.wait_ge(down_done, HSESS * (b + 1))
                A.copy(yT[:, :], pY[:, 0:S]).then_inc(yT_ready, 1)

            def back_copy(b):
                act.wait_ge(back_done, b + 1)
                if b >= 2:
                    act.wait_ge(out_done[b % 2], 16 * (b // 2))
                A.copy(ob[:, b % 2].rearrange("p t d -> p (t d)"), pY[:, 0:S]).then_inc(back_copied, 1)

            def square(b):
                act.wait_ge(y_ready, b + 1)
                A.activation(sq[:, :, :], y[:, :, :, 0:HD].rearrange("p t h d -> p (t h) d"), ACT.Square)\
                    .then_inc(sq_ready, 1)

            square(0)
            ct_high(1)
            q_copy(3)
            values_high(1)
            softplus(1)
            xn_high(0)
            factors(1)
            decay(2)
            for b in range(1, B + 1):
                f = b - 1
                if f >= 1:
                    experts_sum(f - 1)
                if b < B:
                    square(b)
                router_exp(f)
                A.preload_act_table_set("silu_and_others")
                if f >= 1:
                    back_copy(f - 1)
                silu(f, 0)
                cT_high(f)
                silu(f, 1)
                silu(f, 2)
                if b + 1 < B:
                    ct_high(b + 1)
                if b % 2 == 0 and b // 2 + 1 < NG:
                    values_high(b // 2 + 1)
                silu(f, 3)
                silu(f, 4)
                if b < B:
                    A.preload_act_table_set("natural_log_exp_and_others")
                    xn_high(b)
                if b + 2 < B:
                    decay(b + 2)
            experts_sum(B - 1)

        @block.tensor
        def _(pe):
            PAIR = ((0, 0), (1, 0), (0, 1))

            pe.wait_ge(consts_in, 16)

            def turn_ctx(g):
                pe.wait_ge(ctx_in[g], 16)
                for t in range(GRP):
                    ins = pe.transpose(CBANK[g][:, t * P:(t + 1) * P], cx[:, g * GRP + t], ident)
                ins.then_inc(kT_done, 1)

            def turn_q(g):
                pe.wait_ge(q_ready, g + 1)
                for t in range(GRP):
                    ins = pe.transpose(QBANK[g][:, t * P:(t + 1) * P], q[:, g * GRP + t, :], ident)
                ins.then_inc(qT_done, 1)

            def gates(g):
                pe.wait_ge(qT_lo, g + 1)
                pe.wait_ge(kT_lo, g + 1)
                for t in range(g * GRP, (g + 1) * GRP):
                    o = bank[4][:, t * 16:(t + 1) * 16]
                    s = slice(t * P, (t + 1) * P)
                    for j, src in enumerate((qT2, kT2)):
                        for i, (u, v) in enumerate(PAIR):
                            ins = pe.matmul(o, src[:, u, s], wg2[:, v, j],
                                            start=(i + j == 0), stop=(i == 2 and j == 1))
                return ins

            def keep_busy(o, n):
                for i in range(n):
                    pe.matmul(o[:, :], kT2[:, 0, 0:P], kT2[:, 0, 0:512], start=True, stop=True)

            def turn_gates(hf):
                n = hf + 1
                pe.wait_ge(gtok_ready, n)
                for i in range(2):
                    for t in range(TPB):
                        ins = pe.transpose(bank[6][0:n * HR, (i * TPB + t) * P:(i * TPB + t + 1) * P],
                                           gtok[:, i, t, 0:n * HB].rearrange("p b h -> p (b h)"), ident)
                ins.then_inc(gateT_done, 1)

            def turn_factors(hf):
                r = slice(hf * HR, (hf + 1) * HR)
                pe.wait_ge(fac_ready, hf + 1)
                pe.wait_ge(md_ready, hf + 1)
                if hf:
                    pe.wait_ge(tok_ready, hf)
                parts = [gg[r, 0:P], gg[r, P:S], em[r, 0:P], em[r, P:S], wq[r, 0:P], wq[r, P:S],
                         wk[r, 0, 0:P], wk[r, 1, 0:P], wk[r, 2, 0:P], wk[r, 2, P:S]]
                for i, part in enumerate(parts):
                    ins = pe.transpose(bank[7][:, i * HR:(i + 1) * HR], part, ident[r, r])
                ins.then_inc(tokT_done, 1)

            def scores(b, t):
                k = b % 2
                pe.wait_ge(q_in[k], 16 * H * (b // 2 + 1))
                if b == 0:
                    pe.wait_ge(qT_copied, t + 1)
                if b >= 1:
                    pe.wait_ge(ct_ready, TPB * (b - 1) + t + 1)
                for i, (u, v) in enumerate(PAIR):
                    for half in range(2):
                        n = 2 * t + half
                        a = b * S + n * C
                        ins = pe.matmul(pS[t][half * C:(half + 1) * C, :], kT2[:, u, a:a + C],
                                        qblk[:, k, v, :, n * C:(n + 1) * C],
                                        start=(i == 0), stop=(i == 2))
                ins.then_inc(scores_done, 1)

            def states(b):
                k = b % 2
                pe.wait_ge(kw_ready, b + 1)
                if b >= 1:
                    pe.wait_ge(y_ready, b)
                pe.matmul(pC[:, 0:3 * HW], cx[:, b * TPB], kw[:, k, 0:3].rearrange("p n h v -> p (n h v)"),
                          start=True, stop=False)
                pe.matmul(pC[:, 2 * HW:3 * HW], cx[:, b * TPB + 1], kw[:, k, 3].rearrange("p h v -> p (h v)"),
                          start=False, stop=True).then_inc(state_done, 1)

            def intra(b, t, hs):
                k = b % 2
                if t == 0 and hs[0] == 0:
                    pe.wait_ge(ct_lo, b + 1)
                    pe.wait_ge(v_lo, b * TPB // GRP + 1)
                    if b >= 1:
                        pe.wait_ge(y_ready, b)
                for h in hs:
                    for i, (u, v) in enumerate(PAIR):
                        for half in range(2):
                            r = slice(half * C, (half + 1) * C)
                            ins = pe.matmul(pP[r, t * HW + h * VW:t * HW + (h + 1) * VW],
                                            ct2[r, k, u, t, h, :], v2[r, v, b * TPB + t, h, :],
                                            start=(i == 0), stop=(i == 2))
                if hs[-1] == H - 1:
                    ins.then_inc(intra_done, 1)

            LOW, HIGH = range(H // 2), range(H // 2, H)

            def inter(b):
                k = b % 2
                pe.wait_ge(cst_ready, b + 1)
                for n in range(1, NC):
                    t, half = n // 2, n % 2
                    a = b * S + n * C
                    ins = pe.matmul(pC[half * C:(half + 1) * C, t * HW:(t + 1) * HW], qT[:, a:a + C],
                                    cst[:, k, n - 1].rearrange("p h v -> p (h v)"), start=True, stop=True)
                ins.then_inc(inter_done, 1)

            def xn_turn(b):
                pe.wait_ge(xn_ready, b + 1)
                pe.wait_ge(ct_ready, TPB * min(b + 2, B))
                for t in range(TPB):
                    ins = pe.transpose(pX[:, t * P:(t + 1) * P], xn[:, t], ident)
                ins.then_inc(xnT_done, 1)

            def logits(b):
                pe.wait_ge(xnT_lo, b + 1)
                for t in range(TPB):
                    s = slice(t * P, (t + 1) * P)
                    for i, (u, v) in enumerate(PAIR):
                        ins = pe.matmul(pX[:, S + t * (E + 1):S + (t + 1) * (E + 1)], xnT2[:, u, s], wr2[:, v],
                                        start=(i == 0), stop=(i == 2))
                ins.then_inc(logits_done, 1)

            def comb_turn(b):
                pe.wait_ge(comb_ready, b + 1)
                for t in range(TPB):
                    ins = pe.transpose(pX[0:E + 1, S + t * P:S + (t + 1) * P], comb[:, t], ident)
                ins.then_inc(combT_done, 1)

            def hidden(b, s):
                n = HSESS * b + s
                if n >= 2:
                    pe.wait_ge(silu_ready, n - 1)
                    if (n - 2) % HSESS == HSESS - 1:
                        pe.wait_ge(hc_ready, n - 1)
                for j in range(2):
                    for i, (u, v) in enumerate(PAIR):
                        ins = pe.matmul(pH[n % 2][:, j * S:(j + 1) * S], w12[:, u, 2 * s + j], xnT2[:, v],
                                        start=(i == 0), stop=(i == 2))
                ins.then_inc(hid_done, 1)

            def weights(b, s):
                n = HSESS * b + s
                if s == 0:
                    pe.wait_ge(cT_ready, b + 1)
                if n >= 1:
                    pe.wait_ge(hc_ready, n)
                for j in range(2 if s < HSESS - 1 else 1):
                    ins = pe.matmul(pB[:, j * S:(j + 1) * S], sel[:, 2 * s + j], cT2[:, :],
                                    start=True, stop=True)
                ins.then_inc(cb_done, 1)

            def down(b, s):
                n = HSESS * b + s
                pe.wait_ge(hc_ready, n + 1)
                if s == 0 and b >= 1:
                    pe.wait_ge(back_copied, b)
                for j in range(2 if s < HSESS - 1 else 1):
                    e = 2 * s + j
                    ins = pe.matmul(pY[:, 0:S], w2[:, e], hc[:, n % 2, j], start=(e == 0), stop=(e == E))
                ins.then_inc(down_done, 1)

            def back(b):
                pe.wait_ge(yT_ready, b + 1)
                for t in range(TPB):
                    ins = pe.transpose(pY[:, t * P:(t + 1) * P], yT[:, t * P:(t + 1) * P], ident)
                ins.then_inc(back_done, 1)

            turn_ctx(0)
            turn_q(0)
            turn_ctx(1)
            pe.wait_ge(gatew_in, 64)
            for i in range(3):
                ins = pe.transpose(bank[5][:, i * 16:(i + 1) * 16], wg[:, i * D:(i + 1) * D],
                                   ident[0:2 * H, 0:2 * H])
            ins.then_inc(wgT_done, 1)
            turn_q(1)
            pe.wait_ge(kT_lo, 1)
            turn_ctx(2)
            pe.wait_ge(wg_split, 1)
            gates(0)
            gates(1).then_inc(gates_done, 1)
            turn_gates(0)
            scores(0, 0)
            scores(0, 1)
            turn_factors(0)
            turn_q(2)
            turn_ctx(3)
            keep_busy(bank[2], 12)
            states(0)
            scores(1, 0)
            scores(1, 1)
            inter(0)
            intra(0, 0, range(H))
            intra(0, 1, range(H))
            pe.wait_ge(qT_copied, 3)
            turn_q(3)
            states(1)
            keep_busy(bank[2], 3)
            gates(2)
            gates(3).then_inc(gates_done, 1)
            turn_gates(1)
            inter(1)
            intra(1, 0, range(H))
            xn_turn(0)
            intra(1, 1, range(H))
            logits(0)
            pe.wait_ge(w1_lo, 1)
            pe.wait_ge(qT_copied, NG)
            for b in range(1, B + 1):
                f = b - 1
                ahead = b + 1 < B
                hidden(f, 0)
                if b == 1:
                    pe.wait_ge(md_ready, 2)
                hidden(f, 1)
                if b == 1:
                    turn_factors(1)
                if f >= 1:
                    back(f - 1)
                if ahead:
                    scores(b + 1, 0)
                comb_turn(f)
                if ahead:
                    states(b + 1)
                hidden(f, 2)
                if b == 1:
                    pe.wait_ge(tok_ready, 2)
                weights(f, 0)
                if ahead:
                    scores(b + 1, 1)
                hidden(f, 3)
                weights(f, 1)
                down(f, 0)
                weights(f, 2)
                down(f, 1)
                hidden(f, 4)
                if ahead:
                    inter(b + 1)
                if ahead:
                    keep_busy(pS[0], 1)
                weights(f, 3)
                down(f, 2)
                if ahead:
                    intra(b + 1, 0, LOW)
                if b < B:
                    xn_turn(b)
                if ahead:
                    intra(b + 1, 0, HIGH)
                weights(f, 4)
                down(f, 3)
                if ahead:
                    intra(b + 1, 1, LOW)
                if ahead:
                    keep_busy(pS[0], 1)
                down(f, 4)
                if ahead:
                    intra(b + 1, 1, HIGH)
                if b < B:
                    logits(b)
            back(B - 1)

        @block.vector
        def _(dve):
            V = nc.vector
            chain = [0]

            def step(ins):
                chain[0] += 1
                ins.then_inc(dve_chain, 1)
                return chain[0]

            def settle(n=None):
                dve.wait_ge(dve_chain, chain[0] if n is None else n)

            def link(ins):
                step(ins)
                settle()

            def over(ap, n):
                m = ap.shape[1]
                return ap.rearrange("p (m o) -> p m o", o=1).to_broadcast([ap.shape[0], m, n])

            def stats(g):
                dve.wait_ge(x_in[g], 16)
                for t in range(g * GRP, (g + 1) * GRP):
                    ins = step(V.bn_stats(st1[:, t], xs[:, t]))
                return ins

            def moments(g, n):
                settle(n)
                for t in range(g * GRP, (g + 1) * GRP):
                    step(V.bn_aggr(mv1[:, t], st1[:, t]))
                settle()
                s = slice(g * GRP, (g + 1) * GRP)
                V.tensor_scalar(ve1[:, s], mv1[:, s, 1], EPS, None, ALU.add).then_inc(var1_ready, 1)

            def ctx_low(g):
                s = slice(g * GRP * P, (g + 1) * GRP * P)
                dve.wait_ge(kT_hi, g + 1)
                V.tensor_tensor(kT2[:, 1, s], CBANK[g][:, :], kT2[:, 0, s], ALU.subtract).then_inc(kT_lo, 1)

            def q_low(g):
                s = slice(g * GRP * P, (g + 1) * GRP * P)
                dve.wait_ge(qT_hi, g + 1)
                V.tensor_tensor(qT2[:, 1, s], QBANK[g][:, :], qT2[:, 0, s], ALU.subtract)\
                    .then_inc(qT_lo, 1)

            def gate_tokens(hf):
                dve.wait_ge(gates_done, hf + 1)
                src = bank[4][:, 0:2 * H * NT].rearrange("p (b t g h) -> p b t g h", b=B, t=TPB, g=2)
                bs = slice(hf * HB, (hf + 1) * HB)
                for i in range(2):
                    for t in range(TPB):
                        ins = V.tensor_copy(gtok[:, i, t, bs], src[:, bs, t, i, :])
                ins.then_inc(gtok_ready, 1)

            def gate_rows(hf):
                r = slice(hf * HR, (hf + 1) * HR)
                gi, gf = bank[6][r, 0:S], bank[6][r, S:2 * S]
                dve.wait_ge(abs_ready, hf + 1)
                dve.wait_ge(gatew_in, 64)
                link(V.tensor_scalar(mf[r, :], gf, bf[r, :], 0.0, ALU.add, ALU.min))
                dve.wait_ge(ln_ready, hf + 1)
                link(V.tensor_tensor_scan(csum[r, :], mf[r, :], lf[r, :], 0.0, ALU.add, ALU.subtract))
                link(V.scalar_tensor_tensor(gg[r, :], gi, bi[r, :], csum[r, :], ALU.add, ALU.subtract))
                V.tensor_tensor_scan(mm[r, :], gg[r, :], gg[r, :], -3e38, ALU.max, ALU.max)\
                    .then_inc(m_ready, 1)
                dve.wait_ge(m_ready, hf + 1)
                V.tensor_scalar(negR[r, :], mm[r, C - 1::C], -1.0, None, ALU.mult).then_inc(negR_ready, 1)
                V.tensor_tensor(md[r, :], csum[r, :], mm[r, :], ALU.add).then_inc(md_ready, 1)

            def token_factors(hf):
                dve.wait_ge(tokT_done, hf + 1)
                V.tensor_copy(tok[:, :, hf * HB:(hf + 1) * HB].rearrange("p i b h -> p i (b h)"),
                              bank[7][:, 0:10 * HR].rearrange("p (i r) -> p i r", i=10))\
                    .then_inc(tok_ready, 1)
                dve.wait_ge(tok_ready, hf + 1)

            def centre(g):
                dve.wait_ge(ctx_in[g], 16)
                hs, a = slice(g * GRP * H, (g + 1) * GRP * H), slice(g * GRP, (g + 1) * GRP)
                x = cx[:, a].rearrange("p t (h d) -> p (t h) d", h=H)
                link(V.tensor_reduce(vsum[:, hs], x, AX.X, ALU.add))
                V.scalar_tensor_tensor(vc[:, a].rearrange("p t (h d) -> p (t h) d", h=H), over(vsum[:, hs], HD),
                                       -1.0 / HD, x, ALU.mult, ALU.add).then_inc(vc_ready, 1)

            V.memset(qblk[:, 0].rearrange("p a h s -> p (a h s)").bitcast(f32), 0.0).then_inc(zeros_set, 1)
            moments(0, stats(0))
            moments(1, stats(1))
            normalise(dve, 0)
            normalise(dve, 1)
            ctx_low(0)
            q_low(0)
            dve.wait_ge(wgT_done, 1)
            link(V.tensor_copy(wgT[:, :, :].rearrange("p i g -> p (i g)"), bank[5][:, 0:48]))
            step(V.tensor_copy(wgs[:, 0], wgT[:, 0]))
            link(V.tensor_tensor(wgs[:, 1], wgT[:, 1], wgT[:, 2], ALU.add))
            link(V.tensor_copy(wg2[:, 0], wgs[:, :, :]))
            V.tensor_tensor(wg2[:, 1], wgs[:, :, :], wg2[:, 0], ALU.subtract).then_inc(wg_split, 1)
            ctx_low(1)
            q_low(1)
            n = stats(2)
            gate_tokens(0)
            moments(2, n)
            ctx_low(2)
            gate_rows(0)
            centre(0)
            normalise(dve, 2)
            n = stats(3)
            token_factors(0)
            step(mask_tile(V, 0, 1))
            moments(3, n)
            settle()
            dve.wait_ge(m_in[0], 32)
            minus_m(V, 0, slice(1, 2)).then_inc(expo0_ready, 1)
            q_low(2)

            def scores_decay(b, t):
                k = b % 2
                dve.wait_ge(decay_ready, b + 1)
                dve.wait_ge(scores_done, TPB * b + t + 1)
                V.scalar_tensor_tensor(ct[:, k, t].rearrange("p h i -> p (h i)"), pS[t][:, :],
                                       HD ** -0.5, dd[:, k, t].rearrange("p h i -> p (h i)"),
                                       ALU.mult, ALU.mult).then_inc(ct_ready, 1)

            def states(b):
                dve.wait_ge(state_done, b + 1)
                if b >= 2:
                    dve.wait_ge(inter_done, b - 1)
                V.tensor_tensor(cst[:, b % 2].rearrange("p n h v -> p n (h v)"),
                                pC[:, 0:3 * HW].rearrange("p (n m) -> p n m", n=3),
                                mask.rearrange("p (o m) -> p o m", o=1).to_broadcast([P, 3, HW]),
                                ALU.mult).then_inc(cst_ready, 1)

            def sums(b):
                dve.wait_ge(inter_done, b + 1)
                step(V.tensor_tensor(ti[C:P, 0], pC[C:P, 0:HW].rearrange("p (h v) -> p h v", h=H),
                                     over(tok[C:P, T_WQ, b, :], VW), ALU.mult))
                link(V.tensor_tensor(ti[:, 1], pC[:, HW:2 * HW].rearrange("p (h v) -> p h v", h=H),
                                     over(tok[:, T_WQ + 1, b, :], VW), ALU.mult))
                dve.wait_ge(intra_done, TPB * (b + 1))
                V.tensor_tensor(y[:, :].rearrange("p t h v -> p (t h v)"), pP[:, 0:2 * HW],
                                ti[:, :].rearrange("p t h v -> p (t h v)"), ALU.add).then_inc(y_ready, 1)

            def variance(b):
                dve.wait_ge(sq_ready, b + 1)
                link(V.tensor_reduce(vs[:, :], sq[:, :, :], AX.X, ALU.add))
                V.scalar_tensor_tensor(ve[:, :], vs[:, :], 1.0 / HD,
                                       den2[:, :, :].rearrange("p t h -> p (t h)"),
                                       ALU.mult, ALU.add).then_inc(ve_ready, 1)

            def group_norm(b):
                k = b % 2
                dve.wait_ge(rstd_ready, b + 1)
                dve.wait_ge(yw_ready, b + 1)
                dve.wait_ge(xg_ready, b + 1)
                if b >= 2:
                    dve.wait_ge(ob_ready, b - 1)
                link(V.tensor_tensor(yn[:, :, :].rearrange("p t (h d) -> p (t h) d", h=H),
                                     yw[:, :, :].rearrange("p t (h d) -> p (t h) d", h=H),
                                     over(rstd[:, :], HD), ALU.mult))
                V.tensor_tensor(x2[:, k], yn[:, :, :], xg[:, k], ALU.add).then_inc(x2_ready, 1)

            def token_stats(b):
                k = b % 2
                dve.wait_ge(x2_ready, b + 1)
                for t in range(TPB):
                    step(V.bn_stats(st2[:, t], x2[:, k, t]))
                settle()
                for t in range(TPB):
                    step(V.bn_aggr(mv2[:, t], st2[:, t]))
                settle()
                V.tensor_scalar(ve2[:, :], mv2[:, :, 1], EPS, None, ALU.add).then_inc(ve2_ready, 1)

            def layer_norm(b):
                dve.wait_ge(rs2_ready, b + 1)
                if b >= 1:
                    dve.wait_ge(xnT_done, b)
                for t in range(TPB):
                    ins = V.tensor_scalar(xn[:, t], x2[:, b % 2, t], mv2[:, t, 0:1], rs2[:, t:t + 1],
                                          ALU.subtract, ALU.mult)
                ins.then_inc(xn_ready, 1)

            def xn_low(b):
                dve.wait_ge(xnT_hi, b + 1)
                V.tensor_tensor(xnT2[:, 1], pX[:, 0:S], xnT2[:, 0], ALU.subtract).then_inc(xnT_lo, 1)

            def den_low(b):
                dve.wait_ge(y_ready, b + 1)
                return step(V.scalar_tensor_tensor(den[:, :, :], y[:, :, :, HD], -1.0,
                                                   tok[:, T_EM:T_EM + TPB, b, :], ALU.mult, ALU.max))

            def den_high(n):
                settle(n)
                return step(V.tensor_tensor(den[:, :, :], y[:, :, :, HD], den[:, :, :], ALU.max))

            def den_guard(n):
                settle(n)
                return step(V.tensor_scalar(den[:, :, :], den[:, :, :], 1e-6, None, ALU.add))

            def den_square(n):
                settle(n)
                return step(V.scalar_tensor_tensor(den2[:, :, :], den[:, :, :], EPS, den[:, :, :],
                                                   ALU.mult, ALU.mult))

            def route(f, b):
                dve.wait_ge(logits_done, f + 1)
                copied = step(V.tensor_copy(lg[:, :, :].rearrange("p t e -> p (t e)"),
                                            pX[:, S:S + TPB * (E + 1)]))
                if b < B:
                    d = den_low(b)
                settle(copied)
                for t in range(TPB):
                    highest = step(V.max(top[:, t], lg[:, t, 0:E]))
                negated = step(V.tensor_scalar(lm[:, :, E], lg[:, :, E], -1.0, None, ALU.mult))
                if b < B:
                    d = den_high(d)
                settle(negated)
                V.tensor_tensor(lm[:, :, 0:E], lg[:, :, 0:E], over(top[:, :, 0], E), ALU.subtract)\
                    .then_inc(lm_ready, 1)
                for t in range(TPB):
                    found = step(V.max_index(tix[:, t], top[:, t], lg[:, t, 0:E]))
                if b < B:
                    d = den_guard(d)
                settle(found)
                it = iota.rearrange("p (o e) -> p o e", o=1).to_broadcast([P, TPB, E])
                step(V.tensor_tensor(eq1[:, :, :], it, over(tix[:, :, 0], E), ALU.is_equal))
                second = step(V.tensor_tensor(eq2[:, :, :], it, over(tix[:, :, 1], E), ALU.is_equal))
                if b < B:
                    den_square(d)
                settle(second)
                chosen = step(V.tensor_tensor(eq1[:, :, :], eq1[:, :, :], eq2[:, :, :], ALU.add))
                dve.wait_ge(ex_ready, f + 1)
                step(V.tensor_reduce(sden[:, :, 0], ex[:, :, 0:E], AX.X, ALU.add))
                summed = step(V.tensor_scalar(sden[:, :, 1], ex[:, :, E], 1.0, None, ALU.add))
                settle(chosen)
                kept = step(V.tensor_tensor(eq1[:, :, :], eq1[:, :, :], ex[:, :, 0:E], ALU.mult))
                settle(summed)
                inverse = step(V.reciprocal(rden[:, :, :], sden[:, :, :]))
                settle(inverse)
                V.tensor_tensor(comb[:, :, 0:E], eq1[:, :, :], over(rden[:, :, 0], E), ALU.mult)
                V.tensor_copy(comb[:, :, E], rden[:, :, 1]).then_inc(comb_ready, 1)

            def cT_low(b):
                dve.wait_ge(cT_hi, b + 1)
                V.tensor_tensor(cT2[32:32 + E + 1, :], pX[0:E + 1, S:2 * S], cT2[0:E + 1, :], ALU.subtract)\
                    .then_inc(cT_ready, 1)

            def weigh(b, s):
                n = HSESS * b + s
                dve.wait_ge(silu_ready, n + 1)
                dve.wait_ge(cb_done, n + 1)
                if n >= 2:
                    dve.wait_ge(down_done, n - 1)
                if s < HSESS - 1:
                    V.tensor_tensor(hc[:, n % 2].rearrange("p e s -> p (e s)"), pB[:, :],
                                    hh[:, n % 2].rearrange("p e s -> p (e s)"), ALU.mult)\
                        .then_inc(hc_ready, 1)
                else:
                    link(V.tensor_tensor(up[:, :], pH[n % 2][:, S:2 * S], hh[:, n % 2, 0], ALU.mult))
                    V.tensor_tensor(hc[:, n % 2, 0], pB[:, 0:S], up[:, :], ALU.mult).then_inc(hc_ready, 1)

            def low_half(b):
                dve.wait_ge(ct_hi, b + 1)
                if b >= 2:
                    dve.wait_ge(intra_done, TPB * (b - 1))
                ct_low(V, b % 2).then_inc(ct_lo, 1)

            for t in range(TPB):
                scores_decay(0, t)
            low_half(0)
            states(0)
            normalise(dve, 3)
            ctx_low(3)
            centre(1)
            sums(0)
            den_square(den_guard(den_high(den_low(0))))
            variance(0)
            for t in range(TPB):
                scores_decay(1, t)
            q_low(3)
            states(1)
            gate_tokens(1)
            low_half(1)
            group_norm(0)
            token_stats(0)
            layer_norm(0)
            gate_rows(1)
            dve.wait_ge(ffn_in, 16 * 5)
            link(V.tensor_copy(wr2[:, 0], wr[:, :]))
            link(V.tensor_tensor(wr2[:, 1], wr[:, :], wr2[:, 0], ALU.subtract))
            xn_low(0)
            for b in range(1, B + 1):
                f = b - 1
                ahead = b + 1 < B
                if b < B:
                    sums(b)
                route(f, b)
                if b < B:
                    variance(b)
                cT_low(f)
                if b == 1:
                    token_factors(1)
                if ahead:
                    scores_decay(b + 1, 0)
                weigh(f, 0)
                if ahead:
                    scores_decay(b + 1, 1)
                    states(b + 1)
                weigh(f, 1)
                if b < B:
                    group_norm(b)
                weigh(f, 2)
                if b < B:
                    token_stats(b)
                if ahead:
                    low_half(b + 1)
                if b < B:
                    layer_norm(b)
                weigh(f, 3)
                if b % 2 == 1 and b // 2 + 2 < NG:
                    centre(b // 2 + 2)
                if b < B:
                    xn_low(b)
                weigh(f, 4)
            k = (B - 1) % 2
            dve.wait_ge(back_done, B)
            dve.wait_ge(out_done[k], 16 * ((B - 1) // 2))
            V.tensor_tensor(ob[:, k], pY[:, 0:S].rearrange("p (t d) -> p t d", t=TPB), x2[:, k], ALU.add)\
                .then_inc(last_ready, 1)


def constants():
    c = np.zeros((P, K_COLS), np.float32)
    p = np.arange(P)
    c[:, K_ID:K_ID + P] = np.eye(P)
    c[:, K_TRI:K_TRI + C] = np.where(np.arange(C)[None, :] < (p % C)[:, None], NEG, 0)
    c[:, K_IOTA:K_IOTA + E] = np.arange(E)
    c[:, K_ONE] = 1
    c[:, K_HALF:K_HALF + TPB * H] = -0.5
    for h in range(H):
        c[h * HD:(h + 1) * HD, K_MASK + h * VW:K_MASK + (h + 1) * VW] = HD ** -0.5
    sel = np.zeros((64, E + 1, P), np.float16)
    for e in range(E + 1):
        sel[e, e] = 1
        sel[32 + e, e] = 1
    return c, sel


def kernel(**inputs):
    import numpy as _np
    import concourse.bacc as _bacc
    from concourse import mybir as _mybir
    from concourse.bass_utils import run_bass_kernel_spmd as _run

    nc = _bacc.Bacc("TRN2", target_bir_lowering=False, num_devices=1)
    a = {k: _np.ascontiguousarray(v) for k, v in inputs.items()}
    const, sel = constants()
    named = [("x", a["x"]), ("ctx", a["ctx_1024"]), ("wi", a["L0_xattn_Wi_w"]), ("wf", a["L0_xattn_Wf_w"]),
             ("bi", _np.tile(a["L0_xattn_Wi_b"], B).reshape(BH, 1)),
             ("bf", _np.tile(a["L0_xattn_Wf_b"], B).reshape(BH, 1)),
             ("gnw", _np.tile(a["L0_xattn_gn_w"], (P, 1))), ("gnb", _np.tile(a["L0_xattn_gn_b"], (P, 1))),
             ("router", a["L0_ffn_router_w"]), ("gate", a["L0_ffn_shared_gate_w"]), ("w1", a["L0_ffn_w1"]),
             ("w2", a["L0_ffn_w2"]), ("gu", a["L0_ffn_shared_gate_up"]), ("down", a["L0_ffn_shared_down"]),
             ("const", const), ("sel", sel)]
    arrays, args = {}, []
    for name, v in named:
        arrays[f"in_{name}"] = v
        args.append(nc.dram_tensor(f"in_{name}", v.shape, _mybir.dt.from_np(v.dtype),
                                   kind="ExternalInput").ap())
    args.append(nc.dram_tensor("m_scratch", (NC, BH, C), _mybir.dt.float32, kind="Internal").ap())
    args.append(nc.dram_tensor("out_0", (B, S, D), _mybir.dt.float32, kind="ExternalOutput").ap())
    xattn_moe(nc, *args)
    r = _run(nc, [arrays], core_ids=[0])
    return r.results[0]["out_0"]
```
